# Optimizing a Trainium2 kernel written in Bass

```python
import numpy as np
import jax
import jax.numpy as jnp

def _softmax(x, axis=-1):
    return jax.nn.softmax(x, axis=axis)
def _gelu(x):
    return jax.nn.gelu(x, approximate=True)
def _silu(x):
    return jax.nn.silu(x)
def _sigmoid(x):
    return jax.nn.sigmoid(x)
def _layernorm(x, axis=-1, eps=1e-5):
    m = jnp.mean(x, axis=axis, keepdims=True)
    v = jnp.var(x, axis=axis, keepdims=True)
    return (x - m) / jnp.sqrt(v + eps)
def _scatter_add(tgt, idx, src, axis=0):
    return tgt.at[idx].add(src)
def _segment_sum(src, seg, n):
    return jax.ops.segment_sum(src, seg, n)

kernel_name = 'mk_conv_preact_d2_conv_nchw8_758457'

def setup_inputs(seed: int = 0):
    np.random.seed(seed)
    _w = jnp.asarray
    def _rec_inputs():
        import jax
        import jax.numpy as jnp
        _gk = jax.random.key(seed)
        x = 1.508e-05 + 1 * jax.random.normal(jax.random.fold_in(_gk, 1), (8, 8, 1024, 1024), jnp.float32)
        return x
    x = _rec_inputs()
    def _L0_conv_setup():
        import jax, jax.numpy as jnp
        from jax import lax
        import numpy as np
        K = 13
        SIGMA = 6.0
        C = 8
        PAD = K // 2

        def _scipy_gaussian_kernel_2d(kernel_size: int, sigma: float) -> np.ndarray:
            radius = int(4.0 * sigma + 0.5)
            x = np.arange(-radius, radius + 1, dtype=np.float64)
            g1d = np.exp(-0.5 / (sigma * sigma) * x * x)
            g1d /= g1d.sum()
            delta = np.zeros(kernel_size, dtype=np.float64)
            delta[kernel_size // 2] = 1.0
            padded = np.pad(delta, radius, mode='symmetric')
            k1d = np.convolve(padded, g1d, mode='valid')
            k2d = np.outer(k1d, k1d)
            return k2d.astype(np.float32)
        key = jax.random.key(seed)
        x = jax.random.normal(key, (8, C, 1024, 1024), dtype=jnp.float32)
        k2d = _scipy_gaussian_kernel_2d(K, SIGMA)
        w = jnp.tile(jnp.asarray(k2d)[None, None], (C, 1, 1, 1))
        return {'x': x, 'w': w}
    _L0_conv_all = _L0_conv_setup()
    _L0_conv_in = {k: v for k, v in _L0_conv_all.items() if k in ('w', )}
    del _L0_conv_all

    def _L1_conv_setup():
        import jax, jax.numpy as jnp
        import numpy as np
        from jax import lax
        TEMPERATURE = 1.0

        def binarize(w, temperature=TEMPERATURE):
            replace = jnp.clip(w, -1.0, 1.0)
            mean = jnp.mean(jnp.abs(w), axis=(-1, -2, -3), keepdims=True)
            binary = jnp.sign(jnp.clip(w / max(temperature, 0.0), -1.0, 1.0))
            return (lax.stop_gradient(binary - replace) + replace) * mean
        key = jax.random.key(seed)
        k1, k2, k3 = jax.random.split(key, 3)
        x = jax.random.normal(k1, (16, 8, 1024, 1024), dtype=jnp.float32)
        weight = jax.random.normal(k2, (8, 8, 3, 3), dtype=jnp.float32)
        bias = jax.random.normal(k3, (8,), dtype=jnp.float32)
        return {'x': x, 'weight': weight, 'bias': bias}
    _L1_conv_all = _L1_conv_setup()
    _L1_conv_in = {k: v for k, v in _L1_conv_all.items() if k in ('weight', 'bias', )}
    del _L1_conv_all

    return {
        "x": x,
        "L0_conv_w": _L0_conv_in["w"],
        "L1_conv_weight": _L1_conv_in["weight"],
        "L1_conv_bias": _L1_conv_in["bias"],
    }

def reference(x, L0_conv_w, L1_conv_weight, L1_conv_bias):
    import jax
    import jax.numpy as jnp
    def _L0_conv_ref(x, w):
        import jax, jax.numpy as jnp
        from jax import lax
        import numpy as np
        K = 13
        SIGMA = 6.0
        C = 8
        PAD = K // 2

        def _scipy_gaussian_kernel_2d(kernel_size: int, sigma: float) -> np.ndarray:
            radius = int(4.0 * sigma + 0.5)
            x = np.arange(-radius, radius + 1, dtype=np.float64)
            g1d = np.exp(-0.5 / (sigma * sigma) * x * x)
            g1d /= g1d.sum()
            delta = np.zeros(kernel_size, dtype=np.float64)
            delta[kernel_size // 2] = 1.0
            padded = np.pad(delta, radius, mode='symmetric')
            k1d = np.convolve(padded, g1d, mode='valid')
            k2d = np.outer(k1d, k1d)
            return k2d.astype(np.float32)
        xp = jnp.pad(x, ((0, 0), (0, 0), (PAD, PAD), (PAD, PAD)), mode='reflect')
        out = lax.conv_general_dilated(xp, w, window_strides=(1, 1), padding='VALID', dimension_numbers=('NCHW', 'OIHW', 'NCHW'), feature_group_count=C)
        return out

    def _L1_conv_ref(x, weight, bias):
        import jax, jax.numpy as jnp
        import numpy as np
        from jax import lax
        TEMPERATURE = 1.0

        def binarize(w, temperature=TEMPERATURE):
            replace = jnp.clip(w, -1.0, 1.0)
            mean = jnp.mean(jnp.abs(w), axis=(-1, -2, -3), keepdims=True)
            binary = jnp.sign(jnp.clip(w / max(temperature, 0.0), -1.0, 1.0))
            return (lax.stop_gradient(binary - replace) + replace) * mean
        w = binarize(weight)
        xp = jnp.pad(x, ((0, 0), (0, 0), (1, 1), (1, 1)), mode='edge')
        out = lax.conv_general_dilated(xp, w, window_strides=(1, 1), padding='VALID', lhs_dilation=(1, 1), rhs_dilation=(1, 1), dimension_numbers=('NCHW', 'OIHW', 'NCHW'), feature_group_count=1)
        return out + bias[None, :, None, None]

    def _gn(v, G=4, eps=1e-5):
        B_, C_, H_, W_ = v.shape
        g = v.reshape(B_, G, C_ // G, H_, W_)
        m = jnp.mean(g, axis=(2, 3, 4), keepdims=True)
        s = jnp.var(g, axis=(2, 3, 4), keepdims=True)
        return ((g - m) / jnp.sqrt(s + eps)).reshape(v.shape)

    def _ln_c(v, eps=1e-6):
        m = jnp.mean(v, axis=1, keepdims=True)
        s = jnp.var(v, axis=1, keepdims=True)
        return (v - m) / jnp.sqrt(s + eps)

    def _ln_t(v, eps=1e-5):
        m = jnp.mean(v, axis=-1, keepdims=True)
        s = jnp.var(v, axis=-1, keepdims=True)
        return (v - m) / jnp.sqrt(s + eps)

    def _to_tokens(v):
        B_, C_, H_, W_ = v.shape
        return v.reshape(B_, C_, H_ * W_).transpose(0, 2, 1)
    def _from_tokens(t, like):
        B_, C_, H_, W_ = like.shape
        return t.transpose(0, 2, 1).reshape(B_, C_, H_, W_)

    x = x + _L0_conv_ref(_gn(x), L0_conv_w)
    x = x + _L1_conv_ref(_gn(x), L1_conv_weight, L1_conv_bias)
    return x


_drawn_inputs = setup_inputs


def setup_inputs(seed=0):
    import zlib

    import numpy as np

    out = dict(_drawn_inputs(seed))
    spreads = {}
    factors = {'L0_conv_w': 24.349}
    for name, (base, spread) in spreads.items():
        noise = np.random.default_rng([zlib.crc32(name.encode()), seed]).standard_normal(out[name].shape)
        drawn = base * np.exp(spread * noise) if base else spread * noise
        out[name] = jnp.asarray(drawn.astype(out[name].dtype))
    for name, factor in factors.items():
        out[name] = (out[name] * factor).astype(out[name].dtype)
    return out
```

```python
B, C, H, W = 8, 8, 1024, 1024
NCH = B * C
GROUP_CH = 2
NG = NCH // GROUP_CH
GPB = C // GROUP_CH
P = 128
K0, PAD0 = 13, 6
RB, CB = 16, 8
A_OUT, J_OUT = H // RB, W // CB
A_IN, J_IN = A_OUT + 1, J_OUT + 2
CH = CB // 2
R_SIDE = RB + K0 - 1
P_SIDE = R_SIDE * CH
P_HALF = RB * CH
NBLK = 2 * 2 + 1
XCOLS = A_IN * J_IN
EDGE = (H * W - (A_IN - 2) * RB * (J_IN - 3) * CB) // P
NCHUNK = 5
CH_A = A_IN // NCHUNK
TILES = 4
A_T = A_OUT // TILES
GSCALE = 16.0
WSCALE = 1024.0
EPS = 1e-5
WIN, STEP = 16, 14
NWIN = -(-H // STEP)
RPB = NWIN * STEP
UNITS = B * NWIN // 2
UPB = NWIN // 2
Q_ROWS = B * RPB + 2
UN = 8


def build(nc, xb, edge, band, w0, centre, band1, w1, bias, gmask, y1, y2):
    from contextlib import ExitStack
    import concourse.bass as bass
    from concourse import mybir

    F32, F16 = mybir.dt.float32, mybir.dt.float16
    ALU, ACT, AX = mybir.AluOpType, mybir.ActivationFunctionType, mybir.AxisListType
    RADD = bass.bass_isa.ReduceOp.add
    ds = bass.ds

    keep = ExitStack()
    ystat = keep.enter_context(nc.sbuf_tensor("ystat", [P, 2 * NG], F32))

    CREDIT = 1

    with ExitStack() as ctx:
        def sb(name, shape, dt=F32):
            return ctx.enter_context(nc.sbuf_tensor(name, shape, dt))

        def sem(name):
            return ctx.enter_context(nc.semaphore(name))

        psum = [ctx.enter_context(nc.psum_tensor(f"acc{s}", [P, 4, 512], F32)) for s in range(2)]
        xs = [sb(f"x{s}", [P, XCOLS]) for s in range(4)]
        nrm = [sb(f"nrm{s}", [P, CH_A * J_IN]) for s in range(2)]
        yst = [sb(f"y1_{s}", [P, 2048]) for s in range(2)]
        edges = [sb(f"edge{s}", [P, GROUP_CH * EDGE]) for s in range(2)]
        bandf = [sb(f"band{s}", [P, NBLK * P]) for s in range(2)]
        wtmp = sb("wtmp", [P, NBLK * P])
        whi = [sb(f"whi{s}", [P, NBLK * P], F16) for s in range(4)]
        wlo = [sb(f"wlo{s}", [P, NBLK * P], F16) for s in range(4)]
        ctr = sb("ctr", [P, NBLK * P])
        side = [sb(f"side{s}", [P, A_T, 2 * J_IN], F16) for s in range(2)]
        wmax = sb("wmax", [P, C])
        w0s = xs[3][:, 0:C * K0 * K0].rearrange("p (c k) -> p c k", c=C)
        zero = xs[2][:, 0:640]
        NBN = 16
        xbn = sb("xbn", [P, (2 * NBN + 1) * 6])
        ybn = sb("ybn", [P, 2 * TILES * 4 * 6])
        mv = sb("mv", [P, 2])
        pool_gate, dve_gate = sb("pool_gate", [P, 4]), sb("dve_gate", [P, 1])
        ymv = sb("ymv", [P, 2])
        credit = sb("credit", [P, 8])
        msum = sb("msum", [P, 1])
        vpart = sb("vpart", [P, 1])
        vsum = sb("vsum", [P, 1])
        dev = sb("dev", [P, 1])
        var = sb("var", [P, 1])
        root = sb("root", [P, 1])
        rroot = sb("rroot", [P, 1])
        twice = sb("twice", [P, 1])
        rsig = sb("rsig", [P, 1])
        sigma = sb("sigma", [P, 1])
        total = sb("total", [P, 1])
        rtot = sb("rtot", [P, 1])
        rtot2 = sb("rtot2", [P, 1])
        mean = [sb(f"mean{s}", [P, 1]) for s in range(2)]
        gain = [sb(f"gain{s}", [P, 1]) for s in range(2)]
        shift = [sb(f"shift{s}", [P, 1]) for s in range(2)]
        unscale = [sb(f"unscale{s}", [P, 1]) for s in range(4)]

        x_loaded = [sem(f"x_loaded{s}") for s in range(4)]
        edge_loaded = [sem(f"edge_loaded{s}") for s in range(2)]
        band_loaded = [sem(f"band_loaded{s}") for s in range(2)]
        const_loaded = sem("const_loaded")
        zero_ready = sem("zero_ready")
        zero_stored = sem("zero_stored")
        wmax_ready = sem("wmax_ready")
        dve_step = sem("dve_step")
        part_mean_ready = sem("part_mean_ready")
        mean_summed = sem("mean_summed")
        part_var_ready = sem("part_var_ready")
        var_summed = sem("var_summed")
        var_ready = sem("var_ready")
        root_ready = sem("root_ready")
        gain_ready = sem("gain_ready")
        band_read = sem("band_read")
        weights_ready = sem("weights_ready")
        norm_ready = sem("norm_ready")
        hi_ready = sem("hi_ready")
        whi_ready = sem("whi_ready")
        split_ready = sem("split_ready")
        side_ready = sem("side_ready")
        tile_done = sem("tile_done")
        evac_done = [sem(f"evac_done{s}") for s in range(2)]
        ystat_done = [sem(f"ystat_done{s}") for s in range(2)]
        yaggr_done = sem("yaggr_done")
        y_stored = [sem(f"y_stored{s}") for s in range(2)]

        xv = [x[:].rearrange("p (a j) -> p a j", a=A_IN) for x in xs]
        parts = [v.bitcast(F16) for v in xv]
        hiv = [v[:, :, 0:J_IN] for v in parts]
        lov = [v[:, :, J_IN:2 * J_IN] for v in parts]

        CHUNKS = {4: range(0, 3), 5: range(3, 5), 6: range(5, 8), 7: range(8, 10)}
        FIRST_STEP = {2: 1, 3: 9}
        PREP_STEPS = 9 + 3 * GROUP_CH

        block = ctx.enter_context(nc.Block())

        @block.sync
        def _(sp):
            def load_group(G, gi, first=False):
                for c in range(GROUP_CH):
                    k, s = GROUP_CH * G + c, (GROUP_CH * gi + c) % 4
                    if not first:
                        sp.wait_ge(tile_done, TILES * (k - 3))
                    sp.dma_start(xs[s][:], xb[ds(k, 1), :, :].rearrange("k p e -> p (k e)")).then_inc(x_loaded[s], 16)
                sp.dma_start(edges[gi % 2][:], edge[ds(G, 1), :, :].rearrange("g p e -> p (g e)")).then_inc(edge_loaded[gi % 2], 16)

            def load_bands(G, gi, first=False):
                for c in range(GROUP_CH):
                    if not first:
                        sp.wait_ge(band_read, GROUP_CH * (G - 1) + c + 1)
                    sp.dma_start(bandf[c][:], band[(GROUP_CH * gi + c) % C]).then_inc(band_loaded[c], 16)

            sp.dma_start(xs[0][:], xb[0]).then_inc(x_loaded[0], 16)
            sp.dma_start(xs[1][:], xb[1]).then_inc(x_loaded[1], 16)
            sp.dma_start(edges[0][:], edge[0]).then_inc(edge_loaded[0], 16)
            sp.dma_start(w0s, w0.partition_broadcast(P)).then_inc(const_loaded, 16)
            sp.dma_start(ctr[:], centre).then_inc(const_loaded, 16)
            load_bands(0, 0, first=True)
            sp.wait_ge(zero_ready, 1)
            for b in range(B):
                rows = y1[:, b * RPB + H + 2:(b + 1) * RPB, :].rearrange("c q w -> c (q w)").rearrange("c (s w) -> c s w", s=16)
                sp.dma_start(rows, zero[:, 0:rows.shape[2]]).then_inc(zero_stored, 16)
            rows = y1[:, B * RPB:B * RPB + 2, :].rearrange("c q w -> c (q w)").rearrange("c (s w) -> c s w", s=16)
            sp.dma_start(rows, zero[:, 0:rows.shape[2]]).then_inc(zero_stored, 16)
            sp.wait_ge(zero_stored, 16 * (B + 1))
            sp.wait_ge(wmax_ready, 1)
            load_group(1, 1, first=True)

            def step(b, gi, has_band, has_x):
                g = GPB * b + gi
                if has_band:
                    load_bands(g + 1, gi + 1)
                for t in range(2 * TILES):
                    c, tc, s = t // TILES, t % TILES, t % 2
                    ch = GROUP_CH * gi + c
                    q = RPB * b + 1 + RB * A_T * tc
                    sp.wait_ge(evac_done[s], CREDIT + 4 * g + t // 2 + 1)
                    rows = y1[ch:ch + 1, ds(q, RB * A_T), :].rearrange("k (a r) w -> (k r) a w", r=RB)
                    rows = rows.rearrange("r a (c j) -> r c a j", c=CB)
                    rows = rows.rearrange("r c a j -> (r c) a j")
                    sp.dma_start(rows, yst[s][:].rearrange("p (a j) -> p a j", a=A_T)).then_inc(y_stored[s], 16)
                    if tc == 0:
                        sp.dma_start(y1[ch, ds(q - 1, 1), :].rearrange("q (c j) -> (q c) j", c=CB),
                                     yst[s][0:CB, 0:J_OUT]).then_inc(y_stored[s], 16)
                    if tc == TILES - 1:
                        sp.dma_start(y1[ch, ds(q + RB * A_T, 1), :].rearrange("q (c j) -> (q c) j", c=CB),
                                     yst[s][P - CB:P, 2048 - J_OUT:2048]).then_inc(y_stored[s], 16)
                if has_x:
                    load_group(g + 2, gi + 2)

            with sp.Fori(0, B - 1) as b:
                for gi in range(GPB):
                    step(b, gi, True, True)
            for gi in range(GPB):
                step(B - 1, gi, gi < 3, gi < 2)
            for s in range(2):
                sp.wait_ge(y_stored[s], CREDIT + 16 * 3 * NCH)

        @block.gpsimd
        def _(pool):
            nc.gpsimd.memset(zero, 0.0).then_inc(zero_ready, 1)
            nc.gpsimd.memset(pool_gate[:], 0.0).then_inc(zero_ready, 1)
            pool.wait_ge(zero_ready, 2)
            with pool.Fori(0, NG) as g:
                pool.wait_ge(part_mean_ready, g + 1)
                nc.gpsimd.tensor_tensor(pool_gate[:, 0:1], pool_gate[:, 1:2], pool_gate[:, 2:3], ALU.add)
                nc.gpsimd.partition_all_reduce(msum[:], mv[:, 0:1], P, RADD).then_inc(mean_summed, 1)
                pool.wait_ge(part_var_ready, g + 1)
                nc.gpsimd.tensor_tensor(pool_gate[:, 0:1], pool_gate[:, 1:2], pool_gate[:, 2:3], ALU.add)
                nc.gpsimd.partition_all_reduce(vsum[:], vpart[:], P, RADD).then_inc(var_summed, 1)

        @block.tensor
        def _(pe):
            with pe.Fori(0, NCH // 4) as i:
                for s in range(4):
                    k = 4 * i + s
                    pe.wait_ge(weights_ready, k + 1)
                    for t in range(TILES):
                        n = TILES * s + t
                        chunks = -(-(A_T * (t + 1) + 1) // CH_A)
                        pe.wait_ge(split_ready, NCHUNK * k + chunks)
                        pe.wait_ge(evac_done[n % 2], CREDIT + 8 * i + n // 2)
                        for blk in range(NBLK):
                            if blk == NBLK - 1:
                                pe.wait_ge(side_ready, 16 * i + n + 1)
                            for wt, part in ((whi, 0), (whi, 1), (wlo, 0)):
                                for bank in range(4):
                                    if blk < NBLK - 1:
                                        a, j = A_T * t + 4 * bank + blk // 2, blk % 2
                                        src = (hiv, lov)[part][s][:, a:a + 4, j:j + J_OUT]
                                        wts = wt[s][:, blk * P:(blk + 1) * P]
                                    else:
                                        j = part * J_IN + 2
                                        src = side[n % 2][0:P_SIDE, 4 * bank:4 * bank + 4, j:j + J_OUT]
                                        wts = wt[s][0:P_SIDE, blk * P:(blk + 1) * P]
                                    mm = nc.tensor.matmul(psum[n % 2][:, bank, :], wts, src,
                                                          start=(blk == 0 and wt is whi and part == 0),
                                                          stop=(blk == NBLK - 1 and wt is wlo))
                        mm.then_inc(tile_done, 1)

        @block.scalar
        def _(act):
            def take_root(G):
                act.wait_ge(var_ready, G + 1)
                nc.scalar.activation(root[:], var[:], ACT.Sqrt).then_inc(root_ready, 1)

            def normalise(G, gi, j):
                s, q = (GROUP_CH * gi + j // NCHUNK) % 4, j % NCHUNK
                if j == 0:
                    act.wait_ge(gain_ready, G + 1)
                if not (isinstance(G, int) and G == 0 and j < 2):
                    act.wait_ge(split_ready, 2 * NCHUNK * G + j - 1)
                src = xs[s][:, q * CH_A * J_IN:(q + 1) * CH_A * J_IN]
                nc.scalar.activation(nrm[j % 2][:], src, ACT.Identity, bias=shift[gi % 2][:],
                                     scale=gain[gi % 2][:]).then_inc(norm_ready, 1)
                act.wait_ge(norm_ready, 2 * NCHUNK * G + j + 1)
                nc.scalar.activation(hiv[s][:, q * CH_A:(q + 1) * CH_A, :],
                                     nrm[j % 2][:].rearrange("p (a j) -> p a j", a=CH_A), ACT.Identity).then_inc(hi_ready, 1)

            def evacuate(g, gi, t):
                c, tc, s = t // TILES, t % TILES, t % 2
                k = GROUP_CH * g + c
                act.wait_ge(tile_done, 8 * g + t + 1)
                act.wait_ge(ystat_done[s], CREDIT + 4 * g + t // 2)
                act.wait_ge(y_stored[s], CREDIT + 48 * k + (0, 0, 32, 16)[tc])
                nc.scalar.activation(yst[s][:], psum[s][:].rearrange("p b e -> p (b e)"), ACT.Identity,
                                     bias=mean[gi % 2][:], scale=unscale[(GROUP_CH * gi + c) % 4][:]).then_inc(evac_done[s], 1)

            take_root(0)
            for j in range(2 * NCHUNK):
                normalise(0, 0, j)

            def step(b, gi, has_next):
                g = GPB * b + gi
                for t in range(2 * TILES):
                    if has_next and t == 2:
                        take_root(g + 1)
                    if has_next:
                        for j in CHUNKS.get(t, ()):
                            normalise(g + 1, gi + 1, j)
                    evacuate(g, gi, t)

            with act.Fori(0, B - 1) as b:
                for gi in range(GPB):
                    step(b, gi, True)
            for gi in range(GPB):
                step(B - 1, gi, gi < GPB - 1)

        @block.vector
        def _(dve):
            def prepare(G, gi, piece, xloads, edge_count):
                count = [FIRST_STEP.get(piece, 0)]

                def link(ins):
                    count[0] += 1
                    ins.then_inc(dve_step, 1)
                    dve.wait_ge(dve_step, PREP_STEPS * G + count[0])

                m, ga, sh = mean[gi % 2], gain[gi % 2], shift[gi % 2]
                if piece in (0, 1):
                    c = piece
                    s = (GROUP_CH * gi + c) % 4
                    dve.wait_ge(x_loaded[s], 16 * xloads)
                    for n in range(NBN):
                        a0, a1 = 1 + 4 * n, min(1 + 4 * (n + 1), A_IN - 1)
                        nc.vector.bn_stats(xbn[:, (c * NBN + n) * 6:(c * NBN + n + 1) * 6],
                                           xv[s][:, a0:a1, 1:J_IN - 2])
                    if c == 1:
                        dve.wait_ge(edge_loaded[gi % 2], 16 * edge_count)
                        link(nc.vector.bn_stats(xbn[:, 2 * NBN * 6:], edges[gi % 2][:]))
                        nc.vector.memset(dve_gate[:], 0.0)
                        nc.vector.bn_aggr(mv[:], xbn[:]).then_inc(part_mean_ready, 1)
                if piece == 2:
                    dve.wait_ge(mean_summed, G + 1)
                    link(nc.vector.tensor_scalar(m[:], msum[:], 1.0 / P, None, ALU.mult))
                    link(nc.vector.tensor_tensor(dev[:], mv[:, 0:1], m[:], ALU.subtract))
                    nc.vector.scalar_tensor_tensor(out=vpart[:], in0=dev[:], scalar=dev[:], in1=mv[:, 1:2],
                                                   op0=ALU.mult, op1=ALU.add).then_inc(part_var_ready, 1)
                    dve.wait_ge(var_summed, G + 1)
                    nc.vector.tensor_scalar(var[:], vsum[:], 1.0 / P, EPS, ALU.mult, ALU.add).then_inc(var_ready, 1)
                    dve.wait_ge(root_ready, G + 1)
                    link(nc.vector.reciprocal(rroot[:], root[:]))
                    link(nc.vector.scalar_tensor_tensor(out=twice[:], in0=var[:], scalar=rroot[:], in1=root[:],
                                                        op0=ALU.mult, op1=ALU.add))
                    link(nc.vector.tensor_scalar(sigma[:], twice[:], 0.5, None, ALU.mult))
                    link(nc.vector.reciprocal(rsig[:], sigma[:]))
                    link(nc.vector.tensor_scalar(ga[:], rsig[:], GSCALE, None, ALU.mult))
                    link(nc.vector.tensor_scalar(dev[:], m[:], -1.0, None, ALU.mult))
                    nc.vector.tensor_tensor(sh[:], dev[:], ga[:], ALU.mult).then_inc(gain_ready, 1)
                if piece == 3:
                    for c in range(GROUP_CH):
                        ch, slot = (GROUP_CH * gi + c) % C, (GROUP_CH * gi + c) % 4
                        link(nc.vector.tensor_tensor(total[:], wmax[:, ch:ch + 1], sigma[:], ALU.add))
                        nc.vector.tensor_scalar(unscale[slot][:], total[:], 1.0 / (GSCALE * WSCALE), None, ALU.mult)
                        link(nc.vector.reciprocal(rtot[:], total[:]))
                        dve.wait_ge(band_loaded[c], 16 * (G + 1))
                        nc.vector.scalar_tensor_tensor(out=wtmp[:], in0=ctr[:], scalar=sigma[:], in1=bandf[c][:],
                                                       op0=ALU.mult, op1=ALU.add).then_inc(band_read, 1)
                        dve.wait_ge(band_read, GROUP_CH * G + c + 1)
                        link(nc.vector.tensor_scalar(wtmp[:], wtmp[:], rtot[:], WSCALE, ALU.mult, ALU.mult))
                        nc.vector.tensor_copy(whi[slot][:], wtmp[:]).then_inc(whi_ready, 1)
                        dve.wait_ge(whi_ready, GROUP_CH * G + c + 1)
                        nc.vector.tensor_tensor(wlo[slot][:], wtmp[:], whi[slot][:], ALU.subtract).then_inc(weights_ready, 1)
                for j in CHUNKS.get(piece, ()):
                    s, q = (GROUP_CH * gi + j // NCHUNK) % 4, j % NCHUNK
                    rows = slice(q * CH_A, (q + 1) * CH_A)
                    src = nrm[j % 2][:].rearrange("p (a j) -> p a j", a=CH_A)
                    dve.wait_ge(hi_ready, 2 * NCHUNK * G + j + 1)
                    nc.vector.tensor_tensor(lov[s][:, rows, :], src, hiv[s][:, rows, :], ALU.subtract)\
                      .then_inc(split_ready, 1)

            def copy_side(gi, t):
                s, a = (GROUP_CH * gi + t // TILES) % 4, A_T * (t % TILES)
                nc.vector.tensor_copy(side[t % 2][0:P_HALF], parts[s][0:P_HALF, a:a + A_T, :])
                nc.vector.tensor_copy(side[t % 2][P_HALF:P_SIDE], parts[s][0:P_SIDE - P_HALF, a + 1:a + A_T + 1, :])\
                  .then_inc(side_ready, 1)

            def y_stats(g, gi, t):
                s = t % 2
                dve.wait_ge(evac_done[s], CREDIT + 4 * g + t // 2 + 1)
                for q in range(4):
                    ins = nc.vector.bn_stats(ybn[:, (4 * t + q) * 6:(4 * t + q + 1) * 6],
                                             yst[s][:, q * 512:(q + 1) * 512])
                ins.then_inc(ystat_done[s], 1)
                if t == 2 * TILES - 1:
                    dve.wait_ge(ystat_done[s], CREDIT + 4 * g + t // 2 + 1)
                    nc.vector.memset(dve_gate[:], 0.0)
                    nc.vector.bn_aggr(ymv[:], ybn[:]).then_inc(yaggr_done, 1)
                    dve.wait_ge(yaggr_done, g + 1)
                    nc.vector.tensor_copy(ystat[:, ds(2 * g, 2)], ymv[:])

            for col, slot_free in enumerate(evac_done + ystat_done + y_stored):
                nc.vector.memset(credit[:, col:col + 1], 0.0).then_inc(slot_free, CREDIT)
            dve.wait_ge(const_loaded, 32)
            nc.vector.tensor_reduce(wmax[:], w0s, AX.X, ALU.max, apply_absolute_value=True).then_inc(wmax_ready, 1)
            dve.wait_ge(wmax_ready, 1)
            for piece in range(2 * TILES):
                prepare(0, 0, piece, 1, 1)
                if piece in (5, 6):
                    if piece == 5:
                        dve.wait_ge(split_ready, NCHUNK)
                    copy_side(0, piece - 5)

            def step(b, gi, has_next):
                g = GPB * b + gi
                for t in range(2 * TILES):
                    if has_next:
                        n = 2 * b + (gi + 1) // 2 + 1
                        prepare(g + 1, gi + 1, t, n, n)
                    y_stats(g, gi, t)
                    if t < 2 * TILES - 2:
                        dve.wait_ge(split_ready, 2 * NCHUNK * g + NCHUNK * ((t + 2) // TILES + 1))
                        copy_side(gi, t + 2)
                    elif has_next:
                        dve.wait_ge(split_ready, 2 * NCHUNK * (g + 1) + NCHUNK)
                        copy_side(gi + 1, t + 2 - 2 * TILES)

            with dve.Fori(0, B - 1) as b:
                for gi in range(GPB):
                    step(b, gi, True)
            for gi in range(GPB):
                step(B - 1, gi, gi < GPB - 1)

    with ExitStack() as ctx:
        def sb(name, shape, dt=F32):
            return ctx.enter_context(nc.sbuf_tensor(name, shape, dt))

        def sem(name):
            return ctx.enter_context(nc.semaphore(name))

        UC = 2 * W
        psum = [ctx.enter_context(nc.psum_tensor(f"acc1_{s}", [P, 4, 512], F32)) for s in range(2)]
        yin = [sb(f"yin{s}", [P, UC]) for s in range(8)]
        nrm = [sb(f"nrm1_{s}", [P, UC]) for s in range(2)]
        JP = J_OUT + 2
        split = [sb(f"split{s}", [P, 2, 2, CB * JP], F16) for s in range(4)]
        conv = [sb(f"conv{s}", [P, UC]) for s in range(2)]
        yout = [sb(f"yout{s}", [P, UC]) for s in range(2)]
        b1f = sb("b1f", [P, 3 * P])
        pos = sb("pos", [P, 3 * P])
        neg = sb("neg", [P, 3 * P])
        sign = sb("sign", [P, 3 * P], F16)
        w1s = sb("w1s", [P, C * 9])
        wneg = sb("wneg", [P, C * 9])
        wabs = sb("wabs", [P, 1])
        oscale = sb("oscale", [P, 1])
        bias_s = sb("bias_s", [P, 1])
        mask = sb("mask", [P, NG])
        ones = sb("ones", [P, UPB])
        credit = sb("credit1", [P, 16])
        pm = sb("pm", [P, NG])
        gm = sb("gm", [P, NG])
        dv = sb("dv", [P, NG])
        dv2 = sb("dv2", [P, NG])
        pv = sb("pv", [P, NG])
        gv = sb("gv", [P, NG])
        vr = sb("vr", [P, NG])
        rt = sb("rt", [P, NG])
        rrt = sb("rrt", [P, NG])
        tw = sb("tw", [P, NG])
        rs = sb("rs", [P, NG])
        sh = sb("sh", [P, NG])
        sel = sb("sel", [P, NG])
        gain_b = sb("gain_b", [P, B])
        shift_b = sb("shift_b", [P, B])
        gain_u = sb("gain_u", [P, UNITS])
        shift_u = sb("shift_u", [P, UNITS])

        const_loaded = sem("l1_const_loaded")
        yin_loaded = [sem(f"yin_loaded{s}") for s in range(8)]
        setup = sem("l1_setup")
        pm_ready = sem("pm_ready")
        gm_ready = sem("gm_ready")
        pv_ready = sem("pv_ready")
        gv_ready = sem("gv_ready")
        vr_ready = sem("vr_ready")
        rt_ready = sem("rt_ready")
        tables_ready = sem("tables_ready")
        norm_ready = sem("l1_norm_ready")
        hi_ready = sem("l1_hi_ready")
        lo_ready = sem("l1_lo_ready")
        split_ready = sem("l1_split_ready")
        conv_done = sem("l1_conv_done")
        evac_done = [sem(f"l1_evac_done{s}") for s in range(2)]
        added = [sem(f"l1_added{s}") for s in range(8)]
        stored = [sem(f"l1_stored{s}") for s in range(2)]

        splitv = [t[:].rearrange("p w h (c j) -> p w h c j", c=CB) for t in split]

        block = ctx.enter_context(nc.Block())

        @block.sync
        def _(sp):
            for src, dst in ((band1, b1f), (w1, w1s), (bias, bias_s), (gmask, mask)):
                sp.dma_start(dst[:], src).then_inc(const_loaded, 16)

            def load(u, s):
                for w in range(2):
                    q = STEP * (2 * u + w)
                    sp.dma_start(yin[s][:, w * W:(w + 1) * W],
                                 y1[:, ds(q, WIN), :].rearrange("c q w -> q c w")).then_inc(yin_loaded[s], 16)

            LEAD = 6
            for u in range(LEAD):
                load(u, u)

            def step(i, last):
                for v in range(UN):
                    u = UN * i + v
                    if not last or v + LEAD < UN:
                        s = (v + LEAD) % UN
                        sp.wait_ge(added[s], CREDIT + i + (v + LEAD) // UN)
                        load(u + LEAD, s)
                    sp.wait_ge(added[v], CREDIT + i + 1)
                    q = 2 * STEP * u
                    sp.dma_start(y2[ds(q, 2 * STEP), :, :].rearrange("(w r) c e -> (r c) w e", w=2),
                                 yout[v % 2][C:P - C, :].rearrange("p (w e) -> p w e", w=2)).then_inc(stored[v % 2], 16)

            with sp.Fori(0, UNITS // UN - 1) as i:
                step(i, False)
            step(UNITS // UN - 1, True)
            for s in range(2):
                sp.wait_ge(stored[s], CREDIT + 16 * UNITS // 2)

        @block.tensor
        def _(pe):
            pe.wait_ge(tables_ready, 1)
            with pe.Fori(0, UNITS // UN) as i:
                for v in range(UN):
                    pe.wait_ge(split_ready, UN * i + v + 1)
                    pe.wait_ge(evac_done[v % 2], CREDIT + 4 * i + v // 2)
                    for tap in (1, 0, 2):
                        wt = sign[:, tap * P:(tap + 1) * P]
                        for win in range(2):
                            for half in range(2):
                                out = psum[v % 2][:, 2 * win + half, :]
                                for part in range(2):
                                    src = splitv[v % 4][:, win, part]
                                    lo, hi = 4 * half, 4 * half + 4
                                    first, lastp = tap == 1 and part == 0, tap == 2 and part == 1
                                    if tap == 0 and half == 0:
                                        nc.tensor.matmul(out[:, J_OUT:], wt, src[:, 0:3, 1:1 + J_OUT],
                                                         start=False, stop=False)
                                        mm = nc.tensor.matmul(out[:, 0:J_OUT], wt, src[:, CB - 1, 0:J_OUT],
                                                              start=False, stop=False)
                                    elif tap == 2 and half == 1:
                                        nc.tensor.matmul(out[:, 0:3 * J_OUT], wt, src[:, 5:8, 1:1 + J_OUT],
                                                         start=False, stop=False)
                                        mm = nc.tensor.matmul(out[:, 3 * J_OUT:], wt, src[:, 0, 2:2 + J_OUT],
                                                              start=False, stop=lastp)
                                    else:
                                        mm = nc.tensor.matmul(out, wt, src[:, lo + tap - 1:hi + tap - 1, 1:1 + J_OUT],
                                                              start=first, stop=lastp)
                    mm.then_inc(conv_done, 1)

        @block.gpsimd
        def _(pool):
            pool.wait_ge(pm_ready, 1)
            nc.gpsimd.partition_all_reduce(gm[:], pm[:], P, RADD).then_inc(gm_ready, 1)
            pool.wait_ge(pv_ready, 1)
            nc.gpsimd.partition_all_reduce(gv[:], pv[:], P, RADD).then_inc(gv_ready, 1)
            with pool.Fori(0, UNITS // UN) as i:
                for v in range(UN):
                    pool.wait_ge(evac_done[v % 2], CREDIT + 4 * i + v // 2 + 1)
                    pool.wait_ge(stored[v % 2], CREDIT + 16 * (4 * i + v // 2))
                    nc.gpsimd.tensor_tensor(yout[v % 2][:], conv[v % 2][:], yin[v][:], ALU.add).then_inc(added[v], 1)

        @block.scalar
        def _(act):
            act.wait_ge(vr_ready, 1)
            nc.scalar.activation(rt[:], vr[:], ACT.Sqrt).then_inc(rt_ready, 1)
            act.wait_ge(tables_ready, 1)

            def normalise(u, i, v):
                act.wait_ge(yin_loaded[v], 32 * (i + 1))
                if not (isinstance(u, int) and u < 2):
                    act.wait_ge(split_ready, u - 1)
                nc.scalar.activation(nrm[v % 2][:], yin[v][:], ACT.Identity, bias=shift_u[:, ds(u, 1)],
                                     scale=gain_u[:, ds(u, 1)]).then_inc(norm_ready, 1)

            normalise(0, 0, 0)
            normalise(1, 0, 1)

            def step(i, last):
                for v in range(UN):
                    u = UN * i + v
                    if not last or v + 2 < UN:
                        normalise(u + 2, i + (v + 2) // UN, (v + 2) % UN)
                    act.wait_ge(conv_done, u + 1)
                    if v < 2:
                        act.wait_ge(added[UN - 2 + v], CREDIT + i)
                    else:
                        act.wait_ge(added[v - 2], CREDIT + i + 1)
                    nc.scalar.activation(conv[v % 2][:], psum[v % 2][:].rearrange("p b e -> p (b e)"), ACT.Identity,
                                         bias=bias_s[:], scale=oscale[:]).then_inc(evac_done[v % 2], 1)

            with act.Fori(0, UNITS // UN - 1) as i:
                step(i, False)
            step(UNITS // UN - 1, True)

        @block.vector
        def _(dve):
            n = [0]

            def link(ins):
                n[0] += 1
                ins.then_inc(setup, 1)
                dve.wait_ge(setup, n[0])

            for col, slot_free in enumerate(added + evac_done + stored):
                nc.vector.memset(credit[:, col:col + 1], 0.0).then_inc(slot_free, CREDIT)
            dve.wait_ge(const_loaded, 64)
            st = ystat[:].rearrange("p (g m) -> p m g", m=2)
            nc.vector.tensor_copy(pm[:], st[:, 0, :]).then_inc(pm_ready, 1)
            nc.vector.tensor_scalar(pos[:], b1f[:], 0.0, None, ALU.is_gt)
            link(nc.vector.tensor_scalar(neg[:], b1f[:], 0.0, None, ALU.is_lt))
            nc.vector.tensor_tensor(sign[:], pos[:], neg[:], ALU.subtract)
            nc.vector.tensor_reduce(wabs[:], w1s[:], AX.X, ALU.add, apply_absolute_value=True).then_inc(setup, 1)
            n[0] += 1
            dve.wait_ge(setup, n[0])
            link(nc.vector.tensor_scalar(oscale[:], wabs[:], 1.0 / (C * 9 * GSCALE), None, ALU.mult))
            dve.wait_ge(gm_ready, 1)
            link(nc.vector.tensor_scalar(gm[:], gm[:], 1.0 / P, None, ALU.mult))
            link(nc.vector.tensor_tensor(dv[:], pm[:], gm[:], ALU.subtract))
            link(nc.vector.tensor_tensor(dv2[:], dv[:], dv[:], ALU.mult))
            nc.vector.tensor_tensor(pv[:], dv2[:], st[:, 1, :], ALU.add).then_inc(pv_ready, 1)
            dve.wait_ge(gv_ready, 1)
            nc.vector.tensor_scalar(vr[:], gv[:], 1.0 / P, EPS, ALU.mult, ALU.add).then_inc(vr_ready, 1)
            dve.wait_ge(rt_ready, 1)
            link(nc.vector.reciprocal(rrt[:], rt[:]))
            link(nc.vector.tensor_tensor(tw[:], vr[:], rrt[:], ALU.mult))
            link(nc.vector.tensor_tensor(rrt[:], tw[:], rt[:], ALU.add))
            link(nc.vector.tensor_scalar(tw[:], rrt[:], 0.5 / GSCALE, None, ALU.mult))
            link(nc.vector.reciprocal(rs[:], tw[:]))
            link(nc.vector.tensor_tensor(sh[:], gm[:], rs[:], ALU.mult))
            link(nc.vector.tensor_tensor(sel[:], rs[:], mask[:], ALU.mult))
            link(nc.vector.tensor_reduce(gain_b[:], sel[:].rearrange("p (b g) -> p b g", g=GPB), AX.X, ALU.add))
            link(nc.vector.tensor_tensor(sel[:], sh[:], mask[:], ALU.mult))
            link(nc.vector.tensor_reduce(shift_b[:], sel[:].rearrange("p (b g) -> p b g", g=GPB), AX.X, ALU.add))
            link(nc.vector.memset(ones[:], 1.0))
            for b in range(B):
                cols = slice(b * UPB, (b + 1) * UPB)
                nc.vector.tensor_scalar(gain_u[:, cols], ones[:], gain_b[:, b:b + 1], None, ALU.mult)
                ins = nc.vector.tensor_scalar(shift_u[:, cols], ones[:], shift_b[:, b:b + 1], -1.0, ALU.mult, ALU.mult)
            ins.then_inc(tables_ready, 1)

            with dve.Fori(0, UNITS // UN) as i:
                for v in range(UN):
                    u = UN * i + v
                    dst = splitv[v % 4]
                    dve.wait_ge(norm_ready, u + 1)
                    src = nrm[v % 2][:].rearrange("p (w c j) -> p w c j", w=2, c=CB)
                    nc.vector.tensor_copy(dst[:, :, 0, :, 1:1 + J_OUT], src).then_inc(hi_ready, 1)
                    dve.wait_ge(hi_ready, u + 1)
                    nc.vector.tensor_tensor(dst[:, :, 1, :, 1:1 + J_OUT], src, dst[:, :, 0, :, 1:1 + J_OUT],
                                            ALU.subtract).then_inc(lo_ready, 1)
                    dve.wait_ge(lo_ready, u + 1)
                    nc.vector.tensor_copy(dst[:, :, :, CB - 1, 0:1], dst[:, :, :, 0, 1:2])
                    nc.vector.tensor_copy(dst[:, :, :, 0, J_OUT + 1:J_OUT + 2],
                                          dst[:, :, :, CB - 1, J_OUT:J_OUT + 1]).then_inc(split_ready, 1)
    keep.close()


def layouts(x, w0, w1, bias):
    import numpy as np
    xp = np.pad(x, ((0, 0), (0, 0), (PAD0, PAD0), (PAD0, PAD0)), mode="reflect")
    full = np.zeros((B, C, A_IN * RB, J_IN * CB), x.dtype)
    full[:, :, :H + 2 * PAD0, :W + 2 * PAD0] = xp
    blocks = full.reshape(NCH, A_IN, RB, J_IN, CB)
    blocks = blocks.reshape(NCH, A_IN, RB, J_IN, 2, CH).transpose(0, 4, 2, 5, 1, 3)
    r0, r1, c0, c1 = RB, RB * (A_IN - 1), CB, CB * (J_IN - 2)
    y0, y1, x0, x1 = PAD0, PAD0 + H, PAD0, PAD0 + W
    rest = [xp[:, :, y0:r0, x0:x1], xp[:, :, r1:y1, x0:x1], xp[:, :, r0:r1, x0:c0], xp[:, :, r0:r1, c1:x1]]
    rest = np.concatenate([r.reshape(NCH, -1) for r in rest], axis=1)
    edge = rest.reshape(NG, GROUP_CH, P, EDGE).transpose(0, 2, 1, 3)
    half, r, c4, bi, bj, ro, co = np.meshgrid(*[np.arange(n) for n in (2, RB, CH, 2, 2, RB, CB)], indexing="ij")
    dy, dx = RB * bi + r - ro, CB * bj + CH * half + c4 - co
    whole = [d.reshape(P, 4, P) for d in (dy, dx)]
    r, c4, ro, co = np.meshgrid(*[np.arange(n) for n in (P // CH, CH, RB, CB)], indexing="ij")
    sides = [d.reshape(P, 1, P) for d in (np.where(r < R_SIDE, r - ro, -1), 2 * CB + c4 - co)]
    dy, dx = [np.concatenate([a, b], axis=1) for a, b in zip(whole, sides)]
    ok = (dy >= 0) & (dy < K0) & (dx >= 0) & (dx < K0)
    band = np.zeros((C,) + ok.shape, w0.dtype)
    band[:, ok] = w0[:, 0][:, dy[ok], dx[ok]]
    centre = ((dy == PAD0) & (dx == PAD0)).astype(np.float32)
    ri, ci, tap, ro, co = np.meshgrid(*[np.arange(n) for n in (WIN, C, 3, WIN, C)], indexing="ij")
    dy = ri - ro + 1
    ok = (dy >= 0) & (dy < 3) & (ro >= 1) & (ro <= STEP)
    band1 = np.zeros(ok.shape, w1.dtype)
    band1[ok] = w1[co[ok], ci[ok], dy[ok], tap[ok]]
    gmask = np.tile(np.arange(GPB)[None, :] == (np.arange(P) % C // GROUP_CH)[:, None], (1, B)).astype(np.float32)
    return {
        "xb": blocks.reshape(NCH, P, XCOLS), "edge": edge.reshape(NG, P, GROUP_CH * EDGE),
        "band": band.reshape(C, P, NBLK * P), "w0": w0.reshape(C, K0 * K0),
        "centre": centre.reshape(P, NBLK * P), "band1": band1.reshape(P, 3 * P),
        "w1": np.tile(w1.reshape(C, C * 9), (WIN, 1)), "bias": np.tile(bias.reshape(C, 1), (WIN, 1)),
        "gmask": gmask,
    }


def kernel(x, L0_conv_w, L1_conv_weight, L1_conv_bias):
    import numpy as np
    import concourse.bacc as bacc
    from concourse import mybir
    from concourse.bass_utils import run_bass_kernel_spmd

    nc = bacc.Bacc("TRN2", target_bir_lowering=False, num_devices=1)
    arrays, args = {}, []
    laid = layouts(np.asarray(x), np.asarray(L0_conv_w), np.asarray(L1_conv_weight), np.asarray(L1_conv_bias))
    for name, a in laid.items():
        a = np.ascontiguousarray(a)
        arrays["in_" + name] = a
        args.append(nc.dram_tensor("in_" + name, a.shape, mybir.dt.from_np(a.dtype), kind="ExternalInput").ap())
    F32 = mybir.dt.float32
    y1 = nc.dram_tensor("y1", (C, Q_ROWS, W), F32, kind="ExternalOutput").ap()
    y2 = nc.dram_tensor("y2", (B * RPB, C, W), F32, kind="ExternalOutput").ap()
    build(nc, *args, y1, y2)
    r = run_bass_kernel_spmd(nc, [arrays], core_ids=[0])
    out = np.asarray(r.results[0]["y2"]).reshape(B, RPB, C, CB, J_OUT)[:, :H]
    return np.ascontiguousarray(out.transpose(0, 2, 1, 4, 3)).reshape(B, C, H, W)
```

```python
B, C, H, W = 8, 8, 1024, 1024
NCH = B * C
GROUP_CH = 2
NG = NCH // GROUP_CH
GPB = C // GROUP_CH
P = 128
K0, PAD0 = 13, 6
RB, CB = 16, 8
A_OUT, J_OUT = H // RB, W // CB
A_IN, J_IN = A_OUT + 1, J_OUT + 2
CH = CB // 2
R_SIDE = RB + K0 - 1
P_SIDE = R_SIDE * CH
P_HALF = RB * CH
NBLK = 2 * 2 + 1
XCOLS = A_IN * J_IN
EDGE = (H * W - (A_IN - 2) * RB * (J_IN - 3) * CB) // P
NCHUNK = 5
CH_A = A_IN // NCHUNK
TILES = 4
A_T = A_OUT // TILES
GSCALE = 16.0
WSCALE = 1024.0
EPS = 1e-5
WIN, STEP = 16, 14
NWIN = -(-H // STEP)
RPB = NWIN * STEP
UNITS = B * NWIN // 2
UPB = NWIN // 2
Q_ROWS = B * RPB + 2
UN = 8


def build(nc, xb, edge, band, w0, centre, bias0, band1, w1, bias1, gmask, y1, y2):
    from contextlib import ExitStack
    import concourse.bass as bass
    from concourse import mybir

    F32, F16 = mybir.dt.float32, mybir.dt.float16
    ALU, ACT, AX = mybir.AluOpType, mybir.ActivationFunctionType, mybir.AxisListType
    RADD = bass.bass_isa.ReduceOp.add
    ds = bass.ds

    keep = ExitStack()
    ystat = keep.enter_context(nc.sbuf_tensor("ystat", [P, 2 * NCH], F32))
    bias_c = keep.enter_context(nc.sbuf_tensor("bias_c", [P, NCH], F32))

    CREDIT = 1

    with ExitStack() as ctx:
        def sb(name, shape, dt=F32):
            return ctx.enter_context(nc.sbuf_tensor(name, shape, dt))

        def sem(name):
            return ctx.enter_context(nc.semaphore(name))

        psum = [ctx.enter_context(nc.psum_tensor(f"acc{s}", [P, 4, 512], F32)) for s in range(2)]
        xs = [sb(f"x{s}", [P, XCOLS]) for s in range(4)]
        nrm = [sb(f"nrm{s}", [P, CH_A * J_IN]) for s in range(2)]
        yst = [sb(f"y1_{s}", [P, 2048]) for s in range(2)]
        edges = [sb(f"edge{s}", [P, GROUP_CH * EDGE]) for s in range(2)]
        bandf = [sb(f"band{s}", [P, NBLK * P]) for s in range(2)]
        wtmp = sb("wtmp", [P, NBLK * P])
        whi = [sb(f"whi{s}", [P, NBLK * P], F16) for s in range(4)]
        wlo = [sb(f"wlo{s}", [P, NBLK * P], F16) for s in range(4)]
        ctr = sb("ctr", [P, NBLK * P])
        side = [sb(f"side{s}", [P, A_T, 2 * J_IN], F16) for s in range(2)]
        wmax = sb("wmax", [P, C])
        w0s = xs[3][:, 0:C * K0 * K0].rearrange("p (c k) -> p c k", c=C)
        zero = xs[2][:, 0:640]
        NBN = 16
        xbn = sb("xbn", [P, (2 * NBN + 1) * 6])
        ybn = sb("ybn", [P, 2 * TILES * 4 * 6])
        mv = sb("mv", [P, 2])
        pool_gate, dve_gate = sb("pool_gate", [P, 4]), sb("dve_gate", [P, 1])
        ymv = sb("ymv", [P, 2])
        credit = sb("credit", [P, 8])
        msum = sb("msum", [P, 1])
        vpart = sb("vpart", [P, 1])
        vsum = sb("vsum", [P, 1])
        dev = sb("dev", [P, 1])
        var = sb("var", [P, 1])
        root = sb("root", [P, 1])
        rroot = sb("rroot", [P, 1])
        twice = sb("twice", [P, 1])
        rsig = sb("rsig", [P, 1])
        sigma = sb("sigma", [P, 1])
        total = sb("total", [P, 1])
        rtot = sb("rtot", [P, 1])
        rtot2 = sb("rtot2", [P, 1])
        mean = sb("mean", [P, 1])
        gain = [sb(f"gain{s}", [P, 1]) for s in range(2)]
        shift = [sb(f"shift{s}", [P, 1]) for s in range(2)]
        unscale = [sb(f"unscale{s}", [P, 1]) for s in range(4)]

        level = [sb(f"level{s}", [P, 1]) for s in range(4)]
        PIECES = 4
        piece_rows = [0] + [A_IN - 16 * (PIECES - 1 - n) for n in range(PIECES)]

        piece_loaded = [[sem(f"piece_loaded{c}_{n}") for n in range(PIECES)] for c in range(GROUP_CH)]
        x_loaded = [sem(f"x_loaded{s}") for s in range(4)]
        edge_loaded = [sem(f"edge_loaded{s}") for s in range(2)]
        band_loaded = [sem(f"band_loaded{s}") for s in range(2)]
        const_loaded = sem("const_loaded")
        zero_ready = sem("zero_ready")
        zero_stored = sem("zero_stored")
        wmax_ready = sem("wmax_ready")
        dve_step = sem("dve_step")
        part_mean_ready = sem("part_mean_ready")
        mean_summed = sem("mean_summed")
        part_var_ready = sem("part_var_ready")
        var_summed = sem("var_summed")
        var_ready = sem("var_ready")
        root_ready = sem("root_ready")
        gain_ready = sem("gain_ready")
        band_read = sem("band_read")
        weights_ready = sem("weights_ready")
        norm_ready = sem("norm_ready")
        hi_ready = sem("hi_ready")
        whi_ready = sem("whi_ready")
        split_ready = sem("split_ready")
        side_ready = sem("side_ready")
        tile_done = sem("tile_done")
        evac_done = [sem(f"evac_done{s}") for s in range(2)]
        ystat_done = [sem(f"ystat_done{s}") for s in range(2)]
        yaggr_done = sem("yaggr_done")
        y_stored = [sem(f"y_stored{s}") for s in range(2)]

        xv = [x[:].rearrange("p (a j) -> p a j", a=A_IN) for x in xs]
        parts = [v.bitcast(F16) for v in xv]
        hiv = [v[:, :, 0:J_IN] for v in parts]
        lov = [v[:, :, J_IN:2 * J_IN] for v in parts]

        CHUNKS = {4: range(0, 3), 5: range(3, 5), 6: range(5, 8), 7: range(8, 10)}
        FIRST_STEP = {2: 1, 3: 9}
        PREP_STEPS = 9 + 3 * GROUP_CH

        block = ctx.enter_context(nc.Block())

        @block.sync
        def _(sp):
            def load_group(G, gi, first=False):
                for c in range(GROUP_CH):
                    k, s = GROUP_CH * G + c, (GROUP_CH * gi + c) % 4
                    if not first:
                        sp.wait_ge(tile_done, TILES * (k - 3))
                    sp.dma_start(xs[s][:], xb[ds(k, 1), :, :].rearrange("k p e -> p (k e)")).then_inc(x_loaded[s], 16)
                sp.dma_start(edges[gi % 2][:], edge[ds(G, 1), :, :].rearrange("g p e -> p (g e)")).then_inc(edge_loaded[gi % 2], 16)

            def load_bands(G, gi, first=False):
                for c in range(GROUP_CH):
                    if not first:
                        sp.wait_ge(band_read, GROUP_CH * (G - 1) + c + 1)
                    sp.dma_start(bandf[c][:], band[(GROUP_CH * gi + c) % C]).then_inc(band_loaded[c], 16)

            def load_pieces(c):
                for n in range(PIECES):
                    cols = slice(piece_rows[n] * J_IN, piece_rows[n + 1] * J_IN)
                    sp.dma_start(xs[c][:, cols], xb[c, :, cols]).then_inc(piece_loaded[c][n], 16)

            load_pieces(0)
            sp.dma_start(w0s, w0.partition_broadcast(P)).then_inc(const_loaded, 16)
            sp.dma_start(ctr[:], centre).then_inc(const_loaded, 16)
            sp.dma_start(bias_c[:], bias0).then_inc(const_loaded, 16)
            load_bands(0, 0, first=True)
            sp.dma_start(edges[0][:], edge[0]).then_inc(edge_loaded[0], 16)
            load_pieces(1)
            sp.wait_ge(zero_ready, 1)
            for b in range(B):
                rows = y1[:, b * RPB + H + 2:(b + 1) * RPB, :].rearrange("c q w -> c (q w)").rearrange("c (s w) -> c s w", s=16)
                sp.dma_start(rows, zero[:, 0:rows.shape[2]]).then_inc(zero_stored, 16)
            rows = y1[:, B * RPB:B * RPB + 2, :].rearrange("c q w -> c (q w)").rearrange("c (s w) -> c s w", s=16)
            sp.dma_start(rows, zero[:, 0:rows.shape[2]]).then_inc(zero_stored, 16)
            sp.wait_ge(zero_stored, 16 * (B + 1))
            sp.wait_ge(wmax_ready, 1)
            load_group(1, 1, first=True)

            def step(b, gi, has_band, has_x):
                g = GPB * b + gi
                if has_band:
                    load_bands(g + 1, gi + 1)
                for t in range(2 * TILES):
                    c, tc, s = t // TILES, t % TILES, t % 2
                    ch = GROUP_CH * gi + c
                    q = RPB * b + 1 + RB * A_T * tc
                    sp.wait_ge(evac_done[s], CREDIT + 4 * g + t // 2 + 1)
                    rows = y1[ch:ch + 1, ds(q, RB * A_T), :].rearrange("k (a r) w -> (k r) a w", r=RB)
                    rows = rows.rearrange("r a (c j) -> r c a j", c=CB)
                    rows = rows.rearrange("r c a j -> (r c) a j")
                    sp.dma_start(rows, yst[s][:].rearrange("p (a j) -> p a j", a=A_T)).then_inc(y_stored[s], 16)
                    if tc == 0:
                        sp.dma_start(y1[ch, ds(q - 1, 1), :].rearrange("q (c j) -> (q c) j", c=CB),
                                     yst[s][0:CB, 0:J_OUT]).then_inc(y_stored[s], 16)
                    if tc == TILES - 1:
                        sp.dma_start(y1[ch, ds(q + RB * A_T, 1), :].rearrange("q (c j) -> (q c) j", c=CB),
                                     yst[s][P - CB:P, 2048 - J_OUT:2048]).then_inc(y_stored[s], 16)
                if has_x:
                    load_group(g + 2, gi + 2)

            with sp.Fori(0, B - 1) as b:
                for gi in range(GPB):
                    step(b, gi, True, True)
            for gi in range(GPB):
                step(B - 1, gi, gi < 3, gi < 2)
            for s in range(2):
                sp.wait_ge(y_stored[s], CREDIT + 16 * 3 * NCH)

        @block.gpsimd
        def _(pool):
            nc.gpsimd.memset(zero, 0.0).then_inc(zero_ready, 1)
            nc.gpsimd.memset(pool_gate[:], 0.0).then_inc(zero_ready, 1)
            pool.wait_ge(zero_ready, 2)
            with pool.Fori(0, NG) as g:
                pool.wait_ge(part_mean_ready, g + 1)
                nc.gpsimd.tensor_tensor(pool_gate[:, 0:1], pool_gate[:, 1:2], pool_gate[:, 2:3], ALU.add)
                nc.gpsimd.partition_all_reduce(msum[:], mv[:, 0:1], P, RADD).then_inc(mean_summed, 1)
                pool.wait_ge(part_var_ready, g + 1)
                nc.gpsimd.tensor_tensor(pool_gate[:, 0:1], pool_gate[:, 1:2], pool_gate[:, 2:3], ALU.add)
                nc.gpsimd.partition_all_reduce(vsum[:], vpart[:], P, RADD).then_inc(var_summed, 1)

        @block.tensor
        def _(pe):
            with pe.Fori(0, NCH // 4) as i:
                for s in range(4):
                    k = 4 * i + s
                    pe.wait_ge(weights_ready, k + 1)
                    for t in range(TILES):
                        n = TILES * s + t
                        chunks = -(-(A_T * (t + 1) + 1) // CH_A)
                        pe.wait_ge(split_ready, NCHUNK * k + chunks)
                        pe.wait_ge(evac_done[n % 2], CREDIT + 8 * i + n // 2)
                        for blk in range(NBLK):
                            if blk == NBLK - 1:
                                pe.wait_ge(side_ready, 16 * i + n + 1)
                            for wt, part in ((whi, 0), (whi, 1), (wlo, 0)):
                                for bank in range(4):
                                    if blk < NBLK - 1:
                                        a, j = A_T * t + 4 * bank + blk // 2, blk % 2
                                        src = (hiv, lov)[part][s][:, a:a + 4, j:j + J_OUT]
                                        wts = wt[s][:, blk * P:(blk + 1) * P]
                                    else:
                                        j = part * J_IN + 2
                                        src = side[n % 2][0:P_SIDE, 4 * bank:4 * bank + 4, j:j + J_OUT]
                                        wts = wt[s][0:P_SIDE, blk * P:(blk + 1) * P]
                                    mm = nc.tensor.matmul(psum[n % 2][:, bank, :], wts, src,
                                                          start=(blk == 0 and wt is whi and part == 0),
                                                          stop=(blk == NBLK - 1 and wt is wlo))
                        mm.then_inc(tile_done, 1)

        @block.scalar
        def _(act):
            def take_root(G):
                act.wait_ge(var_ready, G + 1)
                nc.scalar.activation(root[:], var[:], ACT.Sqrt).then_inc(root_ready, 1)

            def normalise(G, gi, j):
                s, q = (GROUP_CH * gi + j // NCHUNK) % 4, j % NCHUNK
                if j == 0:
                    act.wait_ge(gain_ready, G + 1)
                if not (isinstance(G, int) and G == 0 and j < 2):
                    act.wait_ge(split_ready, 2 * NCHUNK * G + j - 1)
                src = xs[s][:, q * CH_A * J_IN:(q + 1) * CH_A * J_IN]
                nc.scalar.activation(nrm[j % 2][:], src, ACT.Identity, bias=shift[gi % 2][:],
                                     scale=gain[gi % 2][:]).then_inc(norm_ready, 1)
                act.wait_ge(norm_ready, 2 * NCHUNK * G + j + 1)
                nc.scalar.activation(hiv[s][:, q * CH_A:(q + 1) * CH_A, :],
                                     nrm[j % 2][:].rearrange("p (a j) -> p a j", a=CH_A), ACT.Identity).then_inc(hi_ready, 1)

            def evacuate(g, gi, t):
                c, tc, s = t // TILES, t % TILES, t % 2
                k = GROUP_CH * g + c
                act.wait_ge(tile_done, 8 * g + t + 1)
                act.wait_ge(ystat_done[s], CREDIT + 4 * g + t // 2)
                act.wait_ge(y_stored[s], CREDIT + 48 * k + (0, 0, 32, 16)[tc])
                nc.scalar.activation(yst[s][:], psum[s][:].rearrange("p b e -> p (b e)"), ACT.Identity,
                                     bias=level[(GROUP_CH * gi + c) % 4][:], scale=unscale[(GROUP_CH * gi + c) % 4][:]).then_inc(evac_done[s], 1)

            take_root(0)
            for j in range(2 * NCHUNK):
                normalise(0, 0, j)

            def step(b, gi, has_next):
                g = GPB * b + gi
                for t in range(2 * TILES):
                    if has_next and t == 2:
                        take_root(g + 1)
                    if has_next:
                        for j in CHUNKS.get(t, ()):
                            normalise(g + 1, gi + 1, j)
                    evacuate(g, gi, t)

            with act.Fori(0, B - 1) as b:
                for gi in range(GPB):
                    step(b, gi, True)
            for gi in range(GPB):
                step(B - 1, gi, gi < GPB - 1)

        @block.vector
        def _(dve):
            def prepare(G, gi, piece, xloads, edge_count):
                count = [FIRST_STEP.get(piece, 0)]

                def link(ins):
                    count[0] += 1
                    ins.then_inc(dve_step, 1)
                    dve.wait_ge(dve_step, PREP_STEPS * G + count[0])

                m, ga, sh = mean, gain[gi % 2], shift[gi % 2]
                if piece in (0, 1):
                    c = piece
                    s = (GROUP_CH * gi + c) % 4
                    if xloads is not None:
                        dve.wait_ge(x_loaded[s], 16 * xloads)
                    for n in range(NBN):
                        if xloads is None and n % 4 == 0:
                            dve.wait_ge(piece_loaded[c][n // 4], 16)
                        a0, a1 = 1 + 4 * n, min(1 + 4 * (n + 1), A_IN - 1)
                        nc.vector.bn_stats(xbn[:, (c * NBN + n) * 6:(c * NBN + n + 1) * 6],
                                           xv[s][:, a0:a1, 1:J_IN - 2])
                    if c == 1:
                        dve.wait_ge(edge_loaded[gi % 2], 16 * edge_count)
                        link(nc.vector.bn_stats(xbn[:, 2 * NBN * 6:], edges[gi % 2][:]))
                        nc.vector.memset(dve_gate[:], 0.0)
                        nc.vector.bn_aggr(mv[:], xbn[:]).then_inc(part_mean_ready, 1)
                if piece == 2:
                    dve.wait_ge(mean_summed, G + 1)
                    link(nc.vector.tensor_scalar(m[:], msum[:], 1.0 / P, None, ALU.mult))
                    link(nc.vector.tensor_tensor(dev[:], mv[:, 0:1], m[:], ALU.subtract))
                    nc.vector.scalar_tensor_tensor(out=vpart[:], in0=dev[:], scalar=dev[:], in1=mv[:, 1:2],
                                                   op0=ALU.mult, op1=ALU.add).then_inc(part_var_ready, 1)
                    dve.wait_ge(var_summed, G + 1)
                    nc.vector.tensor_scalar(var[:], vsum[:], 1.0 / P, EPS, ALU.mult, ALU.add).then_inc(var_ready, 1)
                    dve.wait_ge(root_ready, G + 1)
                    link(nc.vector.reciprocal(rroot[:], root[:]))
                    link(nc.vector.scalar_tensor_tensor(out=twice[:], in0=var[:], scalar=rroot[:], in1=root[:],
                                                        op0=ALU.mult, op1=ALU.add))
                    link(nc.vector.tensor_scalar(sigma[:], twice[:], 0.5, None, ALU.mult))
                    link(nc.vector.reciprocal(rsig[:], sigma[:]))
                    link(nc.vector.tensor_scalar(ga[:], rsig[:], GSCALE, None, ALU.mult))
                    link(nc.vector.tensor_scalar(dev[:], m[:], -1.0, None, ALU.mult))
                    nc.vector.tensor_tensor(sh[:], dev[:], ga[:], ALU.mult).then_inc(gain_ready, 1)
                if piece == 3:
                    for c in range(GROUP_CH):
                        ch, slot = (GROUP_CH * gi + c) % C, (GROUP_CH * gi + c) % 4
                        link(nc.vector.tensor_tensor(total[:], wmax[:, ch:ch + 1], sigma[:], ALU.add))
                        nc.vector.tensor_tensor(level[slot][:], mean[:], bias_c[:, ch:ch + 1], ALU.add)
                        nc.vector.tensor_scalar(unscale[slot][:], total[:], 1.0 / (GSCALE * WSCALE), None, ALU.mult)
                        link(nc.vector.reciprocal(rtot[:], total[:]))
                        dve.wait_ge(band_loaded[c], 16 * (G + 1))
                        nc.vector.scalar_tensor_tensor(out=wtmp[:], in0=ctr[:], scalar=sigma[:], in1=bandf[c][:],
                                                       op0=ALU.mult, op1=ALU.add).then_inc(band_read, 1)
                        dve.wait_ge(band_read, GROUP_CH * G + c + 1)
                        link(nc.vector.tensor_scalar(wtmp[:], wtmp[:], rtot[:], WSCALE, ALU.mult, ALU.mult))
                        nc.vector.tensor_copy(whi[slot][:], wtmp[:]).then_inc(whi_ready, 1)
                        dve.wait_ge(whi_ready, GROUP_CH * G + c + 1)
                        nc.vector.tensor_tensor(wlo[slot][:], wtmp[:], whi[slot][:], ALU.subtract).then_inc(weights_ready, 1)
                for j in CHUNKS.get(piece, ()):
                    s, q = (GROUP_CH * gi + j // NCHUNK) % 4, j % NCHUNK
                    rows = slice(q * CH_A, (q + 1) * CH_A)
                    src = nrm[j % 2][:].rearrange("p (a j) -> p a j", a=CH_A)
                    dve.wait_ge(hi_ready, 2 * NCHUNK * G + j + 1)
                    nc.vector.tensor_tensor(lov[s][:, rows, :], src, hiv[s][:, rows, :], ALU.subtract)\
                      .then_inc(split_ready, 1)

            def copy_side(gi, t):
                s, a = (GROUP_CH * gi + t // TILES) % 4, A_T * (t % TILES)
                nc.vector.tensor_copy(side[t % 2][0:P_HALF], parts[s][0:P_HALF, a:a + A_T, :])
                nc.vector.tensor_copy(side[t % 2][P_HALF:P_SIDE], parts[s][0:P_SIDE - P_HALF, a + 1:a + A_T + 1, :])\
                  .then_inc(side_ready, 1)

            def y_stats(g, gi, t):
                s = t % 2
                dve.wait_ge(evac_done[s], CREDIT + 4 * g + t // 2 + 1)
                for q in range(4):
                    ins = nc.vector.bn_stats(ybn[:, (4 * t + q) * 6:(4 * t + q + 1) * 6],
                                             yst[s][:, q * 512:(q + 1) * 512])
                ins.then_inc(ystat_done[s], 1)
                if t % TILES == TILES - 1:
                    c = t // TILES
                    dve.wait_ge(ystat_done[s], CREDIT + 4 * g + t // 2 + 1)
                    nc.vector.memset(dve_gate[:], 0.0)
                    nc.vector.bn_aggr(ymv[:], ybn[:, c * TILES * 24:(c + 1) * TILES * 24]).then_inc(yaggr_done, 1)
                    dve.wait_ge(yaggr_done, GROUP_CH * g + c + 1)
                    nc.vector.tensor_copy(ystat[:, ds(2 * (GROUP_CH * g + c), 2)], ymv[:])

            for col, slot_free in enumerate(evac_done + ystat_done + y_stored):
                nc.vector.memset(credit[:, col:col + 1], 0.0).then_inc(slot_free, CREDIT)
            for piece in range(2 * TILES):
                if piece == 3:
                    dve.wait_ge(const_loaded, 48)
                    nc.vector.tensor_reduce(wmax[:], w0s, AX.X, ALU.max, apply_absolute_value=True).then_inc(wmax_ready, 1)
                    dve.wait_ge(wmax_ready, 1)
                prepare(0, 0, piece, None, 1)
                if piece in (5, 6):
                    if piece == 5:
                        dve.wait_ge(split_ready, NCHUNK)
                    copy_side(0, piece - 5)

            def step(b, gi, has_next):
                g = GPB * b + gi
                for t in range(2 * TILES):
                    if has_next:
                        n = 2 * b + (gi + 1) // 2 + 1
                        prepare(g + 1, gi + 1, t, n - gi % 2, n)
                    y_stats(g, gi, t)
                    if t < 2 * TILES - 2:
                        dve.wait_ge(split_ready, 2 * NCHUNK * g + NCHUNK * ((t + 2) // TILES + 1))
                        copy_side(gi, t + 2)
                    elif has_next:
                        dve.wait_ge(split_ready, 2 * NCHUNK * (g + 1) + NCHUNK)
                        copy_side(gi + 1, t + 2 - 2 * TILES)

            with dve.Fori(0, B - 1) as b:
                for gi in range(GPB):
                    step(b, gi, True)
            for gi in range(GPB):
                step(B - 1, gi, gi < GPB - 1)

    with ExitStack() as ctx:
        def sb(name, shape, dt=F32):
            return ctx.enter_context(nc.sbuf_tensor(name, shape, dt))

        def sem(name):
            return ctx.enter_context(nc.semaphore(name))

        UC = 2 * W
        psum = [ctx.enter_context(nc.psum_tensor(f"acc1_{s}", [P, 4, 512], F32)) for s in range(2)]
        yin = [sb(f"yin{s}", [P, UC]) for s in range(UN)]
        nrm = [sb(f"nrm1_{s}", [P, UC]) for s in range(2)]
        JP = J_OUT + 2
        split = [sb(f"split{s}", [P, 2, 2, CB * JP], F16) for s in range(4)]
        yout = [sb(f"yout{s}", [P, UC]) for s in range(4)]
        b1f = sb("b1f", [P, 3 * P])
        pos = sb("pos", [P, 3 * P])
        neg = sb("neg", [P, 3 * P])
        sign = sb("sign", [P, 3 * P], F16)
        w1s = sb("w1s", [P, C * 9])
        wabs = sb("wabs", [P, 1])
        oscale = sb("oscale", [P, 1])
        bias_p = sb("bias_p", [P, 1])
        mask = sb("mask", [P, NG])
        ones = sb("ones", [P, UPB])
        credit = sb("credit1", [P, 16])
        pm, cm, dv, dv2, pv, cv = [sb(n, [P, NCH]) for n in ("pm", "cm", "dv", "dv2", "pv", "cv")]
        gm, gms, vr, rt, rrt, tw, tw2, rs, sel, sel2 = [
            sb(n, [P, NG]) for n in ("gm", "gms", "vr", "rt", "rrt", "tw", "tw2", "rs", "sel", "sel2")]
        gv = sb("gv", [P, NG])
        gain_b, mean_b, shift_b = [sb(n, [P, B]) for n in ("gain_b", "mean_b", "shift_b")]
        gain_u, shift_u = [sb(n, [P, UNITS]) for n in ("gain_u", "shift_u")]

        const_loaded = sem("l1_const_loaded")
        yin_loaded = [sem(f"yin_loaded{s}") for s in range(UN)]
        setup = sem("l1_setup")
        pm_ready = sem("pm_ready")
        cm_ready = sem("cm_ready")
        pv_ready = sem("pv_ready")
        cv_ready = sem("cv_ready")
        vr_ready = sem("vr_ready")
        rt_ready = sem("rt_ready")
        tables_ready = sem("tables_ready")
        norm_ready = sem("l1_norm_ready")
        hi_ready = sem("l1_hi_ready")
        lo_ready = sem("l1_lo_ready")
        split_ready = sem("l1_split_ready")
        conv_done = sem("l1_conv_done")
        added = [sem(f"l1_added{s}") for s in range(UN)]
        stored = [sem(f"l1_stored{s}") for s in range(4)]
        SPLIT_CREDIT = 2

        def added_before(v, back, i):
            return added[(v - back) % UN], CREDIT + i + 1 + (v - back) // UN

        splitv = [t[:].rearrange("p w h (c j) -> p w h c j", c=CB) for t in split]

        block = ctx.enter_context(nc.Block())

        @block.sync
        def _(sp):
            def load(u, s):
                for w in range(2):
                    q = STEP * (2 * u + w)
                    sp.dma_start(yin[s][:, w * W:(w + 1) * W],
                                 y1[:, ds(q, WIN), :].rearrange("c q w -> q c w")).then_inc(yin_loaded[s], 16)

            LEAD = 6
            load(0, 0)
            for src, dst in ((band1, b1f), (w1, w1s), (bias1, bias_p), (gmask, mask)):
                sp.dma_start(dst[:], src).then_inc(const_loaded, 16)
            for u in range(1, LEAD):
                load(u, u)

            def step(i, last):
                for v in range(UN):
                    u = UN * i + v
                    if not last or v + LEAD < UN:
                        sp.wait_ge(*added_before(v, UN - LEAD, i))
                        load(u + LEAD, (v + LEAD) % UN)
                    sp.wait_ge(*added_before(v, 0, i))
                    q = 2 * STEP * u
                    sp.dma_start(y2[ds(q, 2 * STEP), :, :].rearrange("(w r) c e -> (r c) w e", w=2),
                                 yout[v % 4][C:P - C, :].rearrange("p (w e) -> p w e", w=2)).then_inc(stored[v % 4], 16)

            with sp.Fori(0, UNITS // UN - 1) as i:
                step(i, False)
            step(UNITS // UN - 1, True)
            for s in range(4):
                sp.wait_ge(stored[s], CREDIT + 16 * UNITS // 4)

        @block.tensor
        def _(pe):
            pe.wait_ge(tables_ready, 1)
            with pe.Fori(0, UNITS // UN) as i:
                for v in range(UN):
                    pe.wait_ge(split_ready, SPLIT_CREDIT + UN * i + v + 1)
                    pe.wait_ge(*added_before(v, 2, i))
                    for tap in (1, 0, 2):
                        wt = sign[:, tap * P:(tap + 1) * P]
                        for win in range(2):
                            for half in range(2):
                                out = psum[v % 2][:, 2 * win + half, :]
                                for part in range(2):
                                    src = splitv[v % 4][:, win, part]
                                    lo, hi = 4 * half, 4 * half + 4
                                    first, lastp = tap == 1 and part == 0, tap == 2 and part == 1
                                    if tap == 0 and half == 0:
                                        nc.tensor.matmul(out[:, J_OUT:], wt, src[:, 0:3, 1:1 + J_OUT],
                                                         start=False, stop=False)
                                        mm = nc.tensor.matmul(out[:, 0:J_OUT], wt, src[:, CB - 1, 0:J_OUT],
                                                              start=False, stop=False)
                                    elif tap == 2 and half == 1:
                                        nc.tensor.matmul(out[:, 0:3 * J_OUT], wt, src[:, 5:8, 1:1 + J_OUT],
                                                         start=False, stop=False)
                                        mm = nc.tensor.matmul(out[:, 3 * J_OUT:], wt, src[:, 0, 2:2 + J_OUT],
                                                              start=False, stop=lastp)
                                    else:
                                        mm = nc.tensor.matmul(out, wt, src[:, lo + tap - 1:hi + tap - 1, 1:1 + J_OUT],
                                                              start=first, stop=lastp)
                    mm.then_inc(conv_done, 1)

        @block.gpsimd
        def _(pool):
            pool.wait_ge(pm_ready, 1)
            nc.gpsimd.partition_all_reduce(cm[:], pm[:], P, RADD).then_inc(cm_ready, 1)
            pool.wait_ge(pv_ready, 1)
            nc.gpsimd.partition_all_reduce(cv[:], pv[:], P, RADD).then_inc(cv_ready, 1)

        @block.scalar
        def _(act):
            act.wait_ge(vr_ready, 1)
            nc.scalar.activation(rt[:], vr[:], ACT.Sqrt).then_inc(rt_ready, 1)
            act.wait_ge(tables_ready, 1)
            with act.Fori(0, UNITS // UN) as i:
                for v in range(UN):
                    u = UN * i + v
                    act.wait_ge(yin_loaded[v], 32 * (i + 1))
                    act.wait_ge(split_ready, SPLIT_CREDIT + u - 1)
                    nc.scalar.activation(nrm[v % 2][:], yin[v][:], ACT.Identity, bias=shift_u[:, ds(u, 1)],
                                         scale=gain_u[:, ds(u, 1)]).then_inc(norm_ready, 1)
                    act.wait_ge(*added_before(v, 4, i))
                    act.wait_ge(norm_ready, u + 1)
                    nc.scalar.activation(splitv[v % 4][:, :, 0, :, 1:1 + J_OUT],
                                         nrm[v % 2][:].rearrange("p (w c j) -> p w c j", w=2, c=CB),
                                         ACT.Identity).then_inc(hi_ready, 1)

        @block.vector
        def _(dve):
            n = [0]

            def link(ins):
                n[0] += 1
                ins.then_inc(setup, 1)
                dve.wait_ge(setup, n[0])

            for col, slot_free in enumerate(added + stored):
                nc.vector.memset(credit[:, col:col + 1], 0.0).then_inc(slot_free, CREDIT)
            nc.vector.memset(credit[:, 15:16], 0.0).then_inc(split_ready, SPLIT_CREDIT)
            st = ystat[:].rearrange("p (k m) -> p m k", m=2)
            nc.vector.tensor_tensor(pm[:], st[:, 0, :], bias_c[:], ALU.subtract).then_inc(pm_ready, 1)
            dve.wait_ge(const_loaded, 64)
            nc.vector.tensor_scalar(pos[:], b1f[:], 0.0, None, ALU.is_gt)
            link(nc.vector.tensor_scalar(neg[:], b1f[:], 0.0, None, ALU.is_lt))
            nc.vector.tensor_tensor(sign[:], pos[:], neg[:], ALU.subtract)
            link(nc.vector.tensor_reduce(wabs[:], w1s[:], AX.X, ALU.add, apply_absolute_value=True))
            link(nc.vector.tensor_scalar(oscale[:], wabs[:], 1.0 / (C * 9 * GSCALE), None, ALU.mult))
            dve.wait_ge(cm_ready, 1)
            pair = lambda t: t[:].rearrange("p (g c) -> p g c", c=GROUP_CH)
            link(nc.vector.tensor_reduce(gms[:], pair(cm), AX.X, ALU.add))
            link(nc.vector.tensor_scalar(gm[:], gms[:], 1.0 / (P * GROUP_CH), None, ALU.mult))
            for c in range(GROUP_CH):
                ins = nc.vector.tensor_tensor(pair(dv)[:, :, c], pair(pm)[:, :, c], gm[:], ALU.subtract)
            link(ins)
            link(nc.vector.tensor_tensor(dv2[:], dv[:], dv[:], ALU.mult))
            nc.vector.tensor_tensor(pv[:], dv2[:], st[:, 1, :], ALU.add).then_inc(pv_ready, 1)
            dve.wait_ge(cv_ready, 1)
            link(nc.vector.tensor_reduce(gv[:], pair(cv), AX.X, ALU.add))
            nc.vector.tensor_scalar(vr[:], gv[:], 1.0 / (P * GROUP_CH), EPS, ALU.mult, ALU.add).then_inc(vr_ready, 1)
            dve.wait_ge(rt_ready, 1)
            link(nc.vector.reciprocal(rrt[:], rt[:]))
            link(nc.vector.tensor_tensor(tw[:], vr[:], rrt[:], ALU.mult))
            link(nc.vector.tensor_tensor(tw2[:], tw[:], rt[:], ALU.add))
            link(nc.vector.tensor_scalar(tw[:], tw2[:], 0.5 / GSCALE, None, ALU.mult))
            link(nc.vector.reciprocal(rs[:], tw[:]))
            nc.vector.tensor_tensor(sel[:], rs[:], mask[:], ALU.mult)
            link(nc.vector.tensor_tensor(sel2[:], gm[:], mask[:], ALU.mult))
            nc.vector.tensor_reduce(gain_b[:], sel[:].rearrange("p (b g) -> p b g", g=GPB), AX.X, ALU.add)
            link(nc.vector.tensor_reduce(mean_b[:], sel2[:].rearrange("p (b g) -> p b g", g=GPB), AX.X, ALU.add))
            link(nc.vector.scalar_tensor_tensor(out=shift_b[:], in0=mean_b[:], scalar=bias_p[:], in1=gain_b[:],
                                                op0=ALU.add, op1=ALU.mult))
            link(nc.vector.memset(ones[:], 1.0))
            for b in range(B):
                cols = slice(b * UPB, (b + 1) * UPB)
                nc.vector.tensor_scalar(gain_u[:, cols], ones[:], gain_b[:, b:b + 1], None, ALU.mult)
                ins = nc.vector.tensor_scalar(shift_u[:, cols], ones[:], shift_b[:, b:b + 1], -1.0, ALU.mult, ALU.mult)
            ins.then_inc(tables_ready, 1)

            def low_part(u, v):
                dve.wait_ge(hi_ready, u + 1)
                src = nrm[v % 2][:].rearrange("p (w c j) -> p w c j", w=2, c=CB)
                dst = splitv[v % 4]
                nc.vector.tensor_tensor(dst[:, :, 1, :, 1:1 + J_OUT], src, dst[:, :, 0, :, 1:1 + J_OUT],
                                        ALU.subtract).then_inc(lo_ready, 1)

            def borders(u, v):
                dst = splitv[v % 4]
                dve.wait_ge(lo_ready, u + 1)
                nc.vector.tensor_copy(dst[:, :, :, CB - 1, 0:1], dst[:, :, :, 0, 1:2])
                nc.vector.tensor_copy(dst[:, :, :, 0, J_OUT + 1:J_OUT + 2],
                                      dst[:, :, :, CB - 1, J_OUT:J_OUT + 1]).then_inc(split_ready, 1)

            for u in range(2):
                low_part(u, u)
                borders(u, u)

            def step(i, last):
                for v in range(UN):
                    u = UN * i + v
                    ahead = not last or v + 2 < UN
                    if ahead:
                        low_part(u + 2, (v + 2) % UN)
                    dve.wait_ge(conv_done, u + 1)
                    dve.wait_ge(stored[v % 4], CREDIT + 16 * (2 * i + v // 4))
                    nc.vector.scalar_tensor_tensor(out=yout[v % 4][:], in0=psum[v % 2][:].rearrange("p b e -> p (b e)"),
                                                   scalar=oscale[:], in1=yin[v][:], op0=ALU.mult, op1=ALU.add)\
                      .then_inc(added[v], 1)
                    if ahead:
                        borders(u + 2, (v + 2) % UN)

            with dve.Fori(0, UNITS // UN - 1) as i:
                step(i, False)
            step(UNITS // UN - 1, True)
    keep.close()


def layouts(x, w0, w1, bias):
    import numpy as np
    xp = np.pad(x, ((0, 0), (0, 0), (PAD0, PAD0), (PAD0, PAD0)), mode="reflect")
    full = np.zeros((B, C, A_IN * RB, J_IN * CB), x.dtype)
    full[:, :, :H + 2 * PAD0, :W + 2 * PAD0] = xp
    blocks = full.reshape(NCH, A_IN, RB, J_IN, CB)
    blocks = blocks.reshape(NCH, A_IN, RB, J_IN, 2, CH).transpose(0, 4, 2, 5, 1, 3)
    r0, r1, c0, c1 = RB, RB * (A_IN - 1), CB, CB * (J_IN - 2)
    y0, y1, x0, x1 = PAD0, PAD0 + H, PAD0, PAD0 + W
    rest = [xp[:, :, y0:r0, x0:x1], xp[:, :, r1:y1, x0:x1], xp[:, :, r0:r1, x0:c0], xp[:, :, r0:r1, c1:x1]]
    rest = np.concatenate([r.reshape(NCH, -1) for r in rest], axis=1)
    edge = rest.reshape(NG, GROUP_CH, P, EDGE).transpose(0, 2, 1, 3)
    half, r, c4, bi, bj, ro, co = np.meshgrid(*[np.arange(n) for n in (2, RB, CH, 2, 2, RB, CB)], indexing="ij")
    dy, dx = RB * bi + r - ro, CB * bj + CH * half + c4 - co
    whole = [d.reshape(P, 4, P) for d in (dy, dx)]
    r, c4, ro, co = np.meshgrid(*[np.arange(n) for n in (P // CH, CH, RB, CB)], indexing="ij")
    sides = [d.reshape(P, 1, P) for d in (np.where(r < R_SIDE, r - ro, -1), 2 * CB + c4 - co)]
    dy, dx = [np.concatenate([a, b], axis=1) for a, b in zip(whole, sides)]
    ok = (dy >= 0) & (dy < K0) & (dx >= 0) & (dx < K0)
    band = np.zeros((C,) + ok.shape, w0.dtype)
    band[:, ok] = w0[:, 0][:, dy[ok], dx[ok]]
    centre = ((dy == PAD0) & (dx == PAD0)).astype(np.float32)
    ri, ci, tap, ro, co = np.meshgrid(*[np.arange(n) for n in (WIN, C, 3, WIN, C)], indexing="ij")
    dy = ri - ro + 1
    ok = (dy >= 0) & (dy < 3) & (ro >= 1) & (ro <= STEP)
    band1 = np.zeros(ok.shape, w1.dtype)
    band1[ok] = w1[co[ok], ci[ok], dy[ok], tap[ok]]
    gmask = np.tile(np.arange(GPB)[None, :] == (np.arange(P) % C // GROUP_CH)[:, None], (1, B)).astype(np.float32)
    return {
        "xb": blocks.reshape(NCH, P, XCOLS), "edge": edge.reshape(NG, P, GROUP_CH * EDGE),
        "band": band.reshape(C, P, NBLK * P), "w0": w0.reshape(C, K0 * K0),
        "centre": centre.reshape(P, NBLK * P),
        "bias0": np.tile(bias, (P, B)), "band1": band1.reshape(P, 3 * P),
        "w1": np.tile(w1.reshape(C, C * 9), (WIN, 1)), "bias1": np.tile(bias.reshape(C, 1), (WIN, 1)),
        "gmask": gmask,
    }


def kernel(x, L0_conv_w, L1_conv_weight, L1_conv_bias):
    import numpy as np
    import concourse.bacc as bacc
    from concourse import mybir
    from concourse.bass_utils import run_bass_kernel_spmd

    nc = bacc.Bacc("TRN2", target_bir_lowering=False, num_devices=1)
    arrays, args = {}, []
    laid = layouts(np.asarray(x), np.asarray(L0_conv_w), np.asarray(L1_conv_weight), np.asarray(L1_conv_bias))
    for name, a in laid.items():
        a = np.ascontiguousarray(a)
        arrays["in_" + name] = a
        args.append(nc.dram_tensor("in_" + name, a.shape, mybir.dt.from_np(a.dtype), kind="ExternalInput").ap())
    F32 = mybir.dt.float32
    y1 = nc.dram_tensor("y1", (C, Q_ROWS, W), F32, kind="ExternalOutput").ap()
    y2 = nc.dram_tensor("y2", (B * RPB, C, W), F32, kind="ExternalOutput").ap()
    build(nc, *args, y1, y2)
    r = run_bass_kernel_spmd(nc, [arrays], core_ids=[0])
    out = np.asarray(r.results[0]["y2"]).reshape(B, RPB, C, CB, J_OUT)[:, :H]
    return np.ascontiguousarray(out.transpose(0, 2, 1, 4, 3)).reshape(B, C, H, W)
```

```python
B, C, H, W = 8, 8, 1024, 1024
NCH = B * C
GROUP_CH = 2
NG = NCH // GROUP_CH
GPB = C // GROUP_CH
P = 128
K0, PAD0 = 13, 6
RB, CB = 16, 8
A_OUT, J_OUT = H // RB, W // CB
A_IN, J_IN = A_OUT + 1, J_OUT + 2
CH = CB // 2
R_SIDE = RB + K0 - 1
P_SIDE = R_SIDE * CH
P_HALF = RB * CH
NBLK = 2 * 2 + 1
XCOLS = A_IN * J_IN
EDGE = (H * W - (A_IN - 2) * RB * (J_IN - 3) * CB) // P
NCHUNK = 5
CH_A = A_IN // NCHUNK
TILES = 4
A_T = A_OUT // TILES
GSCALE = 16.0
WSCALE = 1024.0
EPS = 1e-5
WIN, STEP = 16, 14
NWIN = -(-H // STEP)
RPB = NWIN * STEP
UNITS = B * NWIN // 2
UPB = NWIN // 2
Q_ROWS = B * RPB + 2
UN = 8


def build(nc, xb, edge, band, w0, centre, bias0, band1, w1, bias1, gmask, y1, y2):
    from contextlib import ExitStack
    import concourse.bass as bass
    from concourse import mybir

    F32, F16 = mybir.dt.float32, mybir.dt.float16
    ALU, ACT, AX = mybir.AluOpType, mybir.ActivationFunctionType, mybir.AxisListType
    RADD = bass.bass_isa.ReduceOp.add
    ds = bass.ds

    CREDIT = 1

    with ExitStack() as ctx:
        def sb(name, shape, dt=F32):
            return ctx.enter_context(nc.sbuf_tensor(name, shape, dt))

        def sem(name):
            return ctx.enter_context(nc.semaphore(name))

        psum = [ctx.enter_context(nc.psum_tensor(f"acc{s}", [P, 4, 512], F32)) for s in range(2)]
        xs = [sb(f"x{s}", [P, XCOLS]) for s in range(4)]
        CHUNK, BANDC = CH_A * J_IN, NBLK * P
        work = sb("work", [P, 2 * CHUNK + 2 * BANDC])
        nrm = [work[:, s * CHUNK:(s + 1) * CHUNK] for s in range(2)]
        bandf = [work[:, 2 * CHUNK + s * BANDC:2 * CHUNK + (s + 1) * BANDC] for s in range(2)]
        yst = [sb(f"y1_{s}", [P, 2048]) for s in range(2)]
        edge_buf = sb("edge_buf", [P, 2 * GROUP_CH * EDGE])
        edges = [edge_buf[:, s * GROUP_CH * EDGE:(s + 1) * GROUP_CH * EDGE] for s in range(2)]
        wtmp = sb("wtmp", [P, NBLK * P])
        whi = [sb(f"whi{s}", [P, NBLK * P], F16) for s in range(4)]
        wlo = [sb(f"wlo{s}", [P, NBLK * P], F16) for s in range(4)]
        ctr = sb("ctr", [P, NBLK * P])
        side = [sb(f"side{s}", [P, A_T, 2 * J_IN], F16) for s in range(2)]
        wmax = sb("wmax", [P, C])
        w0s = xs[3][:, 0:C * K0 * K0].rearrange("p (c k) -> p c k", c=C)
        zero = xs[2][:, 0:640]
        ystat = sb("ystat", [P, 2 * NCH])
        bias_c = sb("bias_c", [P, NCH])
        NBN = 16
        xbn = sb("xbn", [P, (2 * NBN + 1) * 6])
        ybn = sb("ybn", [P, 2 * TILES * 4 * 6])
        mv = sb("mv", [P, 2])
        pool_gate, dve_gate = sb("pool_gate", [P, 4]), sb("dve_gate", [P, 1])
        ymv = sb("ymv", [P, 2])
        credit = sb("credit", [P, 24])
        msum = sb("msum", [P, 1])
        vpart = sb("vpart", [P, 1])
        vsum = sb("vsum", [P, 1])
        dev = sb("dev", [P, 1])
        var = sb("var", [P, 1])
        root = sb("root", [P, 1])
        rroot = sb("rroot", [P, 1])
        twice = sb("twice", [P, 1])
        rsig = sb("rsig", [P, 1])
        sigma = sb("sigma", [P, 1])
        total = sb("total", [P, 1])
        rtot = sb("rtot", [P, 1])
        mean = sb("mean", [P, 1])
        gain = [sb(f"gain{s}", [P, 1]) for s in range(2)]
        shift = [sb(f"shift{s}", [P, 1]) for s in range(2)]
        unscale = [sb(f"unscale{s}", [P, 1]) for s in range(4)]

        level = [sb(f"level{s}", [P, 1]) for s in range(4)]
        PIECES = 4
        piece_rows = [0] + [A_IN - 16 * (PIECES - 1 - n) for n in range(PIECES)]

        piece_loaded = [[sem(f"piece_loaded{c}_{n}") for n in range(PIECES)] for c in range(GROUP_CH)]
        x_loaded = [sem(f"x_loaded{s}") for s in range(4)]
        edge_loaded = [sem(f"edge_loaded{s}") for s in range(2)]
        band_loaded = [sem(f"band_loaded{s}") for s in range(2)]
        const_loaded = sem("const_loaded")
        zero_ready = sem("zero_ready")
        zero_stored = sem("zero_stored")
        wmax_ready = sem("wmax_ready")
        dve_step = sem("dve_step")
        part_mean_ready = sem("part_mean_ready")
        mean_summed = sem("mean_summed")
        part_var_ready = sem("part_var_ready")
        var_summed = sem("var_summed")
        var_ready = sem("var_ready")
        root_ready = sem("root_ready")
        gain_ready = sem("gain_ready")
        band_read = sem("band_read")
        weights_ready = sem("weights_ready")
        norm_ready = sem("norm_ready")
        hi_ready = sem("hi_ready")
        whi_ready = sem("whi_ready")
        split_ready = sem("split_ready")
        side_ready = sem("side_ready")
        tile_done = sem("tile_done")
        evac_done = [sem(f"evac_done{s}") for s in range(2)]
        ystat_done = [sem(f"ystat_done{s}") for s in range(2)]
        yaggr_done = sem("yaggr_done")
        ystat_kept = sem("ystat_kept")
        y_stored = [sem(f"y_stored{s}") for s in range(2)]

        xv = [x[:].rearrange("p (a j) -> p a j", a=A_IN) for x in xs]
        parts = [v.bitcast(F16) for v in xv]
        hiv = [v[:, :, 0:J_IN] for v in parts]
        lov = [v[:, :, J_IN:2 * J_IN] for v in parts]

        UC = 2 * W
        JP = J_OUT + 2
        yin = [xs[2 * (s // 4)][:, (s % 4) * UC:(s % 4 + 1) * UC] for s in range(UN)]
        u_nrm = [work[:, s * UC:(s + 1) * UC] for s in range(2)]
        u_parts = [xs[1][:, s * 2 * CB * JP:(s + 1) * 2 * CB * JP].bitcast(F16)
                   .rearrange("p (w h c j) -> p w h c j", w=2, h=2, c=CB) for s in range(4)]
        yout = [xs[3][:, s * UC:(s + 1) * UC] for s in range(4)]
        NB1 = 3 * P
        SETUP0 = C * K0 * K0
        b1f, pos, neg = [xs[3][:, SETUP0 + n * NB1:SETUP0 + (n + 1) * NB1] for n in range(3)]
        sign = sb("sign", [P, NB1], F16)
        w1s = sb("w1s", [P, C * 9])
        wabs = sb("wabs", [P, 1])
        oscale = sb("oscale", [P, 1])
        bias_p = sb("bias_p", [P, 1])
        mask = sb("mask", [P, NG])
        ones = sb("ones", [P, UPB])
        gain_u, shift_u = sb("gain_u", [P, UNITS]), sb("shift_u", [P, UNITS])
        mean_b, shift_b, gain_b = sb("mean_b", [P, B]), sb("shift_b", [P, B]), sb("gain_b", [P, B])
        pm, cm, dv, dv2, pv, cv = [edge_buf[:, n * NCH:(n + 1) * NCH] for n in range(6)]
        gm, gms, vr, rt, rrt, tw, tw2, rs, sel, sel2, gv = [
            edge_buf[:, 6 * NCH + n * NG:6 * NCH + (n + 1) * NG] for n in range(11)]

        yin_loaded = [sem(f"yin_loaded{s}") for s in range(UN)]
        u_step = sem("u_step")
        signs_ready = sem("signs_ready")
        pm_ready, cm_ready, pv_ready, cv_ready = sem("pm_ready"), sem("cm_ready"), sem("pv_ready"), sem("cv_ready")
        vr_ready, rt_ready, tables_ready = sem("vr_ready"), sem("rt_ready"), sem("tables_ready")
        u_norm_ready, u_hi_ready, u_lo_ready = sem("u_norm_ready"), sem("u_hi_ready"), sem("u_lo_ready")
        u_split_ready = sem("u_split_ready")
        u_conv_done = sem("u_conv_done")
        added = [sem(f"added{s}") for s in range(UN)]
        stored = [sem(f"stored{s}") for s in range(4)]
        SPLIT_CREDIT = 2
        EARLY = B - 1
        PASSES = UNITS // UN

        def added_before(v, back, i):
            return added[(v - back) % UN], CREDIT + i + 1 + (v - back) // UN

        CHUNKS = {4: range(0, 3), 5: range(3, 5), 6: range(5, 8), 7: range(8, 10)}
        FIRST_STEP = {2: 1, 3: 9}
        PREP_STEPS = 9 + 3 * GROUP_CH

        block = ctx.enter_context(nc.Block())

        @block.sync
        def _(sp):
            def load_group(G, gi, first=False):
                for c in range(GROUP_CH):
                    k, s = GROUP_CH * G + c, (GROUP_CH * gi + c) % 4
                    if not first:
                        sp.wait_ge(tile_done, TILES * (k - 3))
                    sp.dma_start(xs[s][:], xb[ds(k, 1), :, :].rearrange("k p e -> p (k e)")).then_inc(x_loaded[s], 16)
                sp.dma_start(edges[gi % 2], edge[ds(G, 1), :, :].rearrange("g p e -> p (g e)")).then_inc(edge_loaded[gi % 2], 16)

            def load_bands(G, gi, first=False):
                for c in range(GROUP_CH):
                    if not first:
                        sp.wait_ge(band_read, GROUP_CH * (G - 1) + c + 1)
                    sp.dma_start(bandf[c], band[(GROUP_CH * gi + c) % C]).then_inc(band_loaded[c], 16)

            def load_pieces(c):
                for n in range(PIECES):
                    cols = slice(piece_rows[n] * J_IN, piece_rows[n + 1] * J_IN)
                    sp.dma_start(xs[c][:, cols], xb[c, :, cols]).then_inc(piece_loaded[c][n], 16)

            load_pieces(0)
            sp.dma_start(w0s, w0.partition_broadcast(P)).then_inc(const_loaded, 16)
            sp.dma_start(ctr[:], centre).then_inc(const_loaded, 16)
            for dst, src in ((bias_c[:], bias0), (b1f, band1), (w1s[:], w1), (bias_p[:], bias1), (mask[:], gmask)):
                sp.dma_start(dst, src).then_inc(const_loaded, 16)
            load_bands(0, 0, first=True)
            sp.dma_start(edges[0], edge[0]).then_inc(edge_loaded[0], 16)
            load_pieces(1)
            sp.wait_ge(zero_ready, 1)
            for b in range(B):
                rows = y1[:, b * RPB + H + 2:(b + 1) * RPB, :].rearrange("c q w -> c (q w)").rearrange("c (s w) -> c s w", s=16)
                sp.dma_start(rows, zero[:, 0:rows.shape[2]]).then_inc(zero_stored, 16)
            rows = y1[:, B * RPB:B * RPB + 2, :].rearrange("c q w -> c (q w)").rearrange("c (s w) -> c s w", s=16)
            sp.dma_start(rows, zero[:, 0:rows.shape[2]]).then_inc(zero_stored, 16)
            sp.wait_ge(zero_stored, 16 * (B + 1))
            sp.wait_ge(signs_ready, 1)
            load_group(1, 1, first=True)

            def load_unit(u, s):
                for w in range(2):
                    q = STEP * (2 * u + w)
                    sp.dma_start(yin[s][:, w * W:(w + 1) * W],
                                 y1[:, ds(q, WIN), :].rearrange("c q w -> q c w")).then_inc(yin_loaded[s], 16)

            def step(b, gi, has_band, has_x):
                g = GPB * b + gi
                if isinstance(g, int) and g == NG - 1:
                    sp.wait_ge(tile_done, TILES * (NCH - 2))
                    for s in range(2):
                        sp.wait_ge(y_stored[s], CREDIT + 48 * C * EARLY)
                    for u in range(4):
                        load_unit(u, u)
                if has_band:
                    load_bands(g + 1, gi + 1)
                for t in range(2 * TILES):
                    c, tc, s = t // TILES, t % TILES, t % 2
                    ch = GROUP_CH * gi + c
                    q = RPB * b + 1 + RB * A_T * tc
                    sp.wait_ge(evac_done[s], CREDIT + 4 * g + t // 2 + 1)
                    rows = y1[ch:ch + 1, ds(q, RB * A_T), :].rearrange("k (a r) w -> (k r) a w", r=RB)
                    rows = rows.rearrange("r a (c j) -> r c a j", c=CB)
                    rows = rows.rearrange("r c a j -> (r c) a j")
                    sp.dma_start(rows, yst[s][:].rearrange("p (a j) -> p a j", a=A_T)).then_inc(y_stored[s], 16)
                    if tc == 0:
                        sp.dma_start(y1[ch, ds(q - 1, 1), :].rearrange("q (c j) -> (q c) j", c=CB),
                                     yst[s][0:CB, 0:J_OUT]).then_inc(y_stored[s], 16)
                    if tc == TILES - 1:
                        sp.dma_start(y1[ch, ds(q + RB * A_T, 1), :].rearrange("q (c j) -> (q c) j", c=CB),
                                     yst[s][P - CB:P, 2048 - J_OUT:2048]).then_inc(y_stored[s], 16)
                if has_x:
                    load_group(g + 2, gi + 2)

            with sp.Fori(0, B - 1) as b:
                for gi in range(GPB):
                    step(b, gi, True, True)
            for gi in range(GPB):
                step(B - 1, gi, gi < 3, gi < 2)
            for s in range(2):
                sp.wait_ge(y_stored[s], CREDIT + 48 * NCH)

            LEAD = 6
            for u in range(4, LEAD):
                load_unit(u, u)

            def unit_step(i, last):
                for v in range(UN):
                    u = UN * i + v
                    if not last or v + LEAD < UN:
                        sp.wait_ge(*added_before(v, UN - LEAD, i))
                        load_unit(u + LEAD, (v + LEAD) % UN)
                    sp.wait_ge(*added_before(v, 0, i))
                    q = 2 * STEP * u
                    sp.dma_start(y2[ds(q, 2 * STEP), :, :].rearrange("(w r) c e -> (r c) w e", w=2),
                                 yout[v % 4][C:P - C, :].rearrange("p (w e) -> p w e", w=2)).then_inc(stored[v % 4], 16)

            with sp.Fori(0, PASSES - 1) as i:
                unit_step(i, False)
            unit_step(PASSES - 1, True)
            for s in range(4):
                sp.wait_ge(stored[s], CREDIT + 16 * UNITS // 4)

        @block.gpsimd
        def _(pool):
            nc.gpsimd.memset(zero, 0.0).then_inc(zero_ready, 1)
            nc.gpsimd.memset(pool_gate[:], 0.0).then_inc(zero_ready, 1)
            pool.wait_ge(zero_ready, 2)
            with pool.Fori(0, NG) as g:
                pool.wait_ge(part_mean_ready, g + 1)
                nc.gpsimd.tensor_tensor(pool_gate[:, 0:1], pool_gate[:, 1:2], pool_gate[:, 2:3], ALU.add)
                nc.gpsimd.partition_all_reduce(msum[:], mv[:, 0:1], P, RADD).then_inc(mean_summed, 1)
                pool.wait_ge(part_var_ready, g + 1)
                nc.gpsimd.tensor_tensor(pool_gate[:, 0:1], pool_gate[:, 1:2], pool_gate[:, 2:3], ALU.add)
                nc.gpsimd.partition_all_reduce(vsum[:], vpart[:], P, RADD).then_inc(var_summed, 1)
            for n, (b0, b1) in enumerate(((0, EARLY), (EARLY, B))):
                cols = slice(b0 * C, b1 * C)
                pool.wait_ge(pm_ready, n + 1)
                nc.gpsimd.partition_all_reduce(cm[:, cols], pm[:, cols], P, RADD).then_inc(cm_ready, 1)
                pool.wait_ge(pv_ready, n + 1)
                nc.gpsimd.partition_all_reduce(cv[:, cols], pv[:, cols], P, RADD).then_inc(cv_ready, 1)

        @block.tensor
        def _(pe):
            with pe.Fori(0, NCH // 4) as i:
                for s in range(4):
                    k = 4 * i + s
                    pe.wait_ge(weights_ready, k + 1)
                    for t in range(TILES):
                        n = TILES * s + t
                        chunks = -(-(A_T * (t + 1) + 1) // CH_A)
                        pe.wait_ge(split_ready, NCHUNK * k + chunks)
                        pe.wait_ge(evac_done[n % 2], CREDIT + 8 * i + n // 2)
                        for blk in range(NBLK):
                            if blk == NBLK - 1:
                                pe.wait_ge(side_ready, 16 * i + n + 1)
                            for wt, part in ((whi, 0), (whi, 1), (wlo, 0)):
                                for bank in range(4):
                                    if blk < NBLK - 1:
                                        a, j = A_T * t + 4 * bank + blk // 2, blk % 2
                                        src = (hiv, lov)[part][s][:, a:a + 4, j:j + J_OUT]
                                        wts = wt[s][:, blk * P:(blk + 1) * P]
                                    else:
                                        j = part * J_IN + 2
                                        src = side[n % 2][0:P_SIDE, 4 * bank:4 * bank + 4, j:j + J_OUT]
                                        wts = wt[s][0:P_SIDE, blk * P:(blk + 1) * P]
                                    mm = nc.tensor.matmul(psum[n % 2][:, bank, :], wts, src,
                                                          start=(blk == 0 and wt is whi and part == 0),
                                                          stop=(blk == NBLK - 1 and wt is wlo))
                        mm.then_inc(tile_done, 1)

            pe.wait_ge(signs_ready, 1)
            for s in range(2):
                pe.wait_ge(evac_done[s], CREDIT + 2 * NCH)
            with pe.Fori(0, PASSES) as i:
                for v in range(UN):
                    pe.wait_ge(u_split_ready, UN * i + v + 1)
                    pe.wait_ge(*added_before(v, 2, i))
                    for tap in (1, 0, 2):
                        wt = sign[:, tap * P:(tap + 1) * P]
                        for win in range(2):
                            for half in range(2):
                                out = psum[v % 2][:, 2 * win + half, :]
                                for part in range(2):
                                    src = u_parts[v % 4][:, win, part]
                                    lo, hi = 4 * half, 4 * half + 4
                                    first, last = tap == 1 and part == 0, tap == 2 and part == 1
                                    if tap == 0 and half == 0:
                                        nc.tensor.matmul(out[:, J_OUT:], wt, src[:, 0:3, 1:1 + J_OUT],
                                                         start=False, stop=False)
                                        mm = nc.tensor.matmul(out[:, 0:J_OUT], wt, src[:, CB - 1, 0:J_OUT],
                                                              start=False, stop=False)
                                    elif tap == 2 and half == 1:
                                        nc.tensor.matmul(out[:, 0:3 * J_OUT], wt, src[:, 5:8, 1:1 + J_OUT],
                                                         start=False, stop=False)
                                        mm = nc.tensor.matmul(out[:, 3 * J_OUT:], wt, src[:, 0, 2:2 + J_OUT],
                                                              start=False, stop=last)
                                    else:
                                        mm = nc.tensor.matmul(out, wt, src[:, lo + tap - 1:hi + tap - 1, 1:1 + J_OUT],
                                                              start=first, stop=last)
                    mm.then_inc(u_conv_done, 1)

        @block.scalar
        def _(act):
            def take_root(G):
                act.wait_ge(var_ready, G + 1)
                nc.scalar.activation(root[:], var[:], ACT.Sqrt).then_inc(root_ready, 1)

            def normalise(G, gi, j):
                s, q = (GROUP_CH * gi + j // NCHUNK) % 4, j % NCHUNK
                if j == 0:
                    act.wait_ge(gain_ready, G + 1)
                if not (isinstance(G, int) and G == 0 and j < 2):
                    act.wait_ge(split_ready, 2 * NCHUNK * G + j - 1)
                src = xs[s][:, q * CH_A * J_IN:(q + 1) * CH_A * J_IN]
                nc.scalar.activation(nrm[j % 2], src, ACT.Identity, bias=shift[gi % 2][:],
                                     scale=gain[gi % 2][:]).then_inc(norm_ready, 1)
                act.wait_ge(norm_ready, 2 * NCHUNK * G + j + 1)
                nc.scalar.activation(hiv[s][:, q * CH_A:(q + 1) * CH_A, :],
                                     nrm[j % 2].rearrange("p (a j) -> p a j", a=CH_A), ACT.Identity).then_inc(hi_ready, 1)

            def evacuate(g, gi, t):
                c, tc, s = t // TILES, t % TILES, t % 2
                k = GROUP_CH * g + c
                act.wait_ge(tile_done, 8 * g + t + 1)
                act.wait_ge(ystat_done[s], CREDIT + 4 * g + t // 2)
                act.wait_ge(y_stored[s], CREDIT + 48 * k + (0, 0, 32, 16)[tc])
                nc.scalar.activation(yst[s][:], psum[s][:].rearrange("p b e -> p (b e)"), ACT.Identity,
                                     bias=level[(GROUP_CH * gi + c) % 4][:], scale=unscale[(GROUP_CH * gi + c) % 4][:]).then_inc(evac_done[s], 1)

            take_root(0)
            for j in range(2 * NCHUNK):
                normalise(0, 0, j)

            def table_root(n, b0, b1):
                act.wait_ge(vr_ready, n + 1)
                cols = slice(b0 * GPB, b1 * GPB)
                nc.scalar.activation(rt[:, cols], vr[:, cols], ACT.Sqrt).then_inc(rt_ready, 1)

            def split_unit(i, v):
                u = UN * i + v
                act.wait_ge(yin_loaded[v], 32 * (i + 1))
                act.wait_ge(u_lo_ready, SPLIT_CREDIT + u - 1)
                nc.scalar.activation(u_nrm[v % 2], yin[v], ACT.Identity, bias=shift_u[:, ds(u, 1)],
                                     scale=gain_u[:, ds(u, 1)]).then_inc(u_norm_ready, 1)
                if not (isinstance(i, int) and u < 4):
                    act.wait_ge(*added_before(v, 4, i))
                act.wait_ge(u_norm_ready, u + 1)
                nc.scalar.activation(u_parts[v % 4][:, :, 0, :, 1:1 + J_OUT],
                                     u_nrm[v % 2].rearrange("p (w c j) -> p w c j", w=2, c=CB),
                                     ACT.Identity).then_inc(u_hi_ready, 1)

            def borders(i, v):
                dst = u_parts[v % 4]
                act.wait_ge(u_lo_ready, SPLIT_CREDIT + UN * i + v + 1)
                nc.scalar.activation(dst[:, :, :, CB - 1, 0:1], dst[:, :, :, 0, 1:2], ACT.Identity)
                nc.scalar.activation(dst[:, :, :, 0, J_OUT + 1:J_OUT + 2],
                                     dst[:, :, :, CB - 1, J_OUT:J_OUT + 1], ACT.Identity).then_inc(u_split_ready, 1)

            def step(b, gi, has_next):
                g = GPB * b + gi
                for t in range(2 * TILES):
                    if not has_next and t == 2:
                        table_root(0, 0, EARLY)
                    if not has_next and t in (5, 6):
                        if t == 5:
                            act.wait_ge(tables_ready, 1)
                            act.wait_ge(split_ready, 2 * NCHUNK * NG)
                        split_unit(0, t - 5)
                        if t == 6:
                            borders(0, 0)
                    if has_next and t == 2:
                        take_root(g + 1)
                    if has_next:
                        for j in CHUNKS.get(t, ()):
                            normalise(g + 1, gi + 1, j)
                    evacuate(g, gi, t)

            with act.Fori(0, B - 1) as b:
                for gi in range(GPB):
                    step(b, gi, True)
            for gi in range(GPB):
                step(B - 1, gi, gi < GPB - 1)

            for v in range(2, UN):
                split_unit(0, v)
                borders(0, v - 1)
                if v == 2:
                    table_root(1, EARLY, B)
            act.wait_ge(tables_ready, 2)
            with act.Fori(1, PASSES) as i:
                for v in range(UN):
                    split_unit(i, v)
                    borders(i - (v == 0), (v - 1) % UN)
            borders(PASSES - 1, UN - 1)

        @block.vector
        def _(dve):
            def linker(G, first):
                count = [first]

                def link(ins):
                    count[0] += 1
                    ins.then_inc(dve_step, 1)
                    dve.wait_ge(dve_step, PREP_STEPS * G + count[0])
                return link

            def weights(G, gi, c):
                link = linker(G, FIRST_STEP[3] + 3 * c)
                ch, slot = (GROUP_CH * gi + c) % C, (GROUP_CH * gi + c) % 4
                link(nc.vector.tensor_tensor(total[:], wmax[:, ch:ch + 1], sigma[:], ALU.add))
                nc.vector.tensor_tensor(level[slot][:], mean[:], bias_c[:, ch:ch + 1], ALU.add)
                nc.vector.tensor_scalar(unscale[slot][:], total[:], 1.0 / (GSCALE * WSCALE), None, ALU.mult)
                link(nc.vector.reciprocal(rtot[:], total[:]))
                dve.wait_ge(band_loaded[c], 16 * (G + 1))
                nc.vector.scalar_tensor_tensor(out=wtmp[:], in0=ctr[:], scalar=sigma[:], in1=bandf[c],
                                               op0=ALU.mult, op1=ALU.add).then_inc(band_read, 1)
                dve.wait_ge(band_read, GROUP_CH * G + c + 1)
                link(nc.vector.tensor_scalar(wtmp[:], wtmp[:], rtot[:], WSCALE, ALU.mult, ALU.mult))
                nc.vector.tensor_copy(whi[slot][:], wtmp[:]).then_inc(whi_ready, 1)
                dve.wait_ge(whi_ready, GROUP_CH * G + c + 1)
                nc.vector.tensor_tensor(wlo[slot][:], wtmp[:], whi[slot][:], ALU.subtract).then_inc(weights_ready, 1)

            def prepare(G, gi, piece, xloads, edge_count, channels=range(GROUP_CH)):
                link = linker(G, FIRST_STEP.get(piece, 0))
                m, ga, sh = mean, gain[gi % 2], shift[gi % 2]
                if piece in (0, 1):
                    c = piece
                    s = (GROUP_CH * gi + c) % 4
                    if xloads is not None:
                        dve.wait_ge(x_loaded[s], 16 * xloads)
                    for n in range(NBN):
                        if xloads is None and n % 4 == 0:
                            dve.wait_ge(piece_loaded[c][n // 4], 16)
                        a0, a1 = 1 + 4 * n, min(1 + 4 * (n + 1), A_IN - 1)
                        nc.vector.bn_stats(xbn[:, (c * NBN + n) * 6:(c * NBN + n + 1) * 6],
                                           xv[s][:, a0:a1, 1:J_IN - 2])
                    if c == 1:
                        dve.wait_ge(edge_loaded[gi % 2], 16 * edge_count)
                        link(nc.vector.bn_stats(xbn[:, 2 * NBN * 6:], edges[gi % 2]))
                        nc.vector.memset(dve_gate[:], 0.0)
                        nc.vector.bn_aggr(mv[:], xbn[:]).then_inc(part_mean_ready, 1)
                if piece == 2:
                    dve.wait_ge(mean_summed, G + 1)
                    link(nc.vector.tensor_scalar(m[:], msum[:], 1.0 / P, None, ALU.mult))
                    link(nc.vector.tensor_tensor(dev[:], mv[:, 0:1], m[:], ALU.subtract))
                    nc.vector.scalar_tensor_tensor(out=vpart[:], in0=dev[:], scalar=dev[:], in1=mv[:, 1:2],
                                                   op0=ALU.mult, op1=ALU.add).then_inc(part_var_ready, 1)
                    dve.wait_ge(var_summed, G + 1)
                    nc.vector.tensor_scalar(var[:], vsum[:], 1.0 / P, EPS, ALU.mult, ALU.add).then_inc(var_ready, 1)
                    dve.wait_ge(root_ready, G + 1)
                    link(nc.vector.reciprocal(rroot[:], root[:]))
                    link(nc.vector.scalar_tensor_tensor(out=twice[:], in0=var[:], scalar=rroot[:], in1=root[:],
                                                        op0=ALU.mult, op1=ALU.add))
                    link(nc.vector.tensor_scalar(sigma[:], twice[:], 0.5, None, ALU.mult))
                    link(nc.vector.reciprocal(rsig[:], sigma[:]))
                    link(nc.vector.tensor_scalar(ga[:], rsig[:], GSCALE, None, ALU.mult))
                    link(nc.vector.tensor_scalar(dev[:], m[:], -1.0, None, ALU.mult))
                    nc.vector.tensor_tensor(sh[:], dev[:], ga[:], ALU.mult).then_inc(gain_ready, 1)
                if piece == 3:
                    for c in channels:
                        weights(G, gi, c)
                for j in CHUNKS.get(piece, ()):
                    s, q = (GROUP_CH * gi + j // NCHUNK) % 4, j % NCHUNK
                    rows = slice(q * CH_A, (q + 1) * CH_A)
                    src = nrm[j % 2].rearrange("p (a j) -> p a j", a=CH_A)
                    dve.wait_ge(hi_ready, 2 * NCHUNK * G + j + 1)
                    nc.vector.tensor_tensor(lov[s][:, rows, :], src, hiv[s][:, rows, :], ALU.subtract)\
                      .then_inc(split_ready, 1)

            def copy_side(gi, t):
                s, a = (GROUP_CH * gi + t // TILES) % 4, A_T * (t % TILES)
                nc.vector.tensor_copy(side[t % 2][0:P_HALF], parts[s][0:P_HALF, a:a + A_T, :])
                nc.vector.tensor_copy(side[t % 2][P_HALF:P_SIDE], parts[s][0:P_SIDE - P_HALF, a + 1:a + A_T + 1, :])\
                  .then_inc(side_ready, 1)

            def y_stats(g, gi, t):
                s = t % 2
                dve.wait_ge(evac_done[s], CREDIT + 4 * g + t // 2 + 1)
                for q in range(4):
                    ins = nc.vector.bn_stats(ybn[:, (4 * t + q) * 6:(4 * t + q + 1) * 6],
                                             yst[s][:, q * 512:(q + 1) * 512])
                ins.then_inc(ystat_done[s], 1)
                if t % TILES == TILES - 1:
                    c = t // TILES
                    dve.wait_ge(ystat_done[s], CREDIT + 4 * g + t // 2 + 1)
                    nc.vector.memset(dve_gate[:], 0.0)
                    nc.vector.bn_aggr(ymv[:], ybn[:, c * TILES * 24:(c + 1) * TILES * 24]).then_inc(yaggr_done, 1)
                    dve.wait_ge(yaggr_done, GROUP_CH * g + c + 1)
                    nc.vector.tensor_copy(ystat[:, ds(2 * (GROUP_CH * g + c), 2)], ymv[:]).then_inc(ystat_kept, 1)

            for col, slot_free in enumerate(evac_done + ystat_done + y_stored + added + stored):
                nc.vector.memset(credit[:, col:col + 1], 0.0).then_inc(slot_free, CREDIT)
            nc.vector.memset(credit[:, 23:24], 0.0).then_inc(u_lo_ready, SPLIT_CREDIT)
            table_steps = [0]

            def table_link(ins):
                table_steps[0] += 1
                ins.then_inc(u_step, 1)
                dve.wait_ge(u_step, table_steps[0])

            def prepare_signs():
                nc.vector.tensor_scalar(pos, b1f, 0.0, None, ALU.is_gt)
                table_link(nc.vector.tensor_scalar(neg, b1f, 0.0, None, ALU.is_lt))
                nc.vector.tensor_tensor(sign[:], pos, neg, ALU.subtract)
                table_link(nc.vector.tensor_reduce(wabs[:], w1s[:], AX.X, ALU.add, apply_absolute_value=True))
                nc.vector.tensor_scalar(oscale[:], wabs[:], 1.0 / (C * 9 * GSCALE), None, ALU.mult)
                nc.vector.memset(ones[:], 1.0).then_inc(signs_ready, 1)

            def tables(n, b0, b1):
                ch, gr, bs = slice(b0 * C, b1 * C), slice(b0 * GPB, b1 * GPB), slice(b0, b1)
                st = ystat[:].rearrange("p (k m) -> p m k", m=2)
                pair = lambda t: t[:, ch].rearrange("p (g c) -> p g c", c=GROUP_CH)
                dve.wait_ge(ystat_kept, C * b1)
                nc.vector.tensor_tensor(pm[:, ch], st[:, 0, ch], bias_c[:, ch], ALU.subtract).then_inc(pm_ready, 1)
                dve.wait_ge(cm_ready, n + 1)
                table_link(nc.vector.tensor_reduce(gms[:, gr], pair(cm), AX.X, ALU.add))
                table_link(nc.vector.tensor_scalar(gm[:, gr], gms[:, gr], 1.0 / (P * GROUP_CH), None, ALU.mult))
                for c in range(GROUP_CH):
                    ins = nc.vector.tensor_tensor(pair(dv)[:, :, c], pair(pm)[:, :, c], gm[:, gr], ALU.subtract)
                table_link(ins)
                table_link(nc.vector.tensor_tensor(dv2[:, ch], dv[:, ch], dv[:, ch], ALU.mult))
                nc.vector.tensor_tensor(pv[:, ch], dv2[:, ch], st[:, 1, ch], ALU.add).then_inc(pv_ready, 1)
                dve.wait_ge(cv_ready, n + 1)
                table_link(nc.vector.tensor_reduce(gv[:, gr], pair(cv), AX.X, ALU.add))
                nc.vector.tensor_scalar(vr[:, gr], gv[:, gr], 1.0 / (P * GROUP_CH), EPS, ALU.mult, ALU.add)\
                  .then_inc(vr_ready, 1)
                dve.wait_ge(rt_ready, n + 1)
                table_link(nc.vector.reciprocal(rrt[:, gr], rt[:, gr]))
                table_link(nc.vector.tensor_tensor(tw[:, gr], vr[:, gr], rrt[:, gr], ALU.mult))
                table_link(nc.vector.tensor_tensor(tw2[:, gr], tw[:, gr], rt[:, gr], ALU.add))
                table_link(nc.vector.tensor_scalar(tw[:, gr], tw2[:, gr], 0.5 / GSCALE, None, ALU.mult))
                table_link(nc.vector.reciprocal(rs[:, gr], tw[:, gr]))
                nc.vector.tensor_tensor(sel[:, gr], rs[:, gr], mask[:, gr], ALU.mult)
                table_link(nc.vector.tensor_tensor(sel2[:, gr], gm[:, gr], mask[:, gr], ALU.mult))
                own = lambda t: t[:, gr].rearrange("p (b g) -> p b g", g=GPB)
                nc.vector.tensor_reduce(gain_b[:, bs], own(sel), AX.X, ALU.add)
                table_link(nc.vector.tensor_reduce(mean_b[:, bs], own(sel2), AX.X, ALU.add))
                table_link(nc.vector.scalar_tensor_tensor(out=shift_b[:, bs], in0=mean_b[:, bs], scalar=bias_p[:],
                                                          in1=gain_b[:, bs], op0=ALU.add, op1=ALU.mult))
                for b in range(b0, b1):
                    cols = slice(b * UPB, (b + 1) * UPB)
                    nc.vector.tensor_scalar(gain_u[:, cols], ones[:], gain_b[:, b:b + 1], None, ALU.mult)
                    ins = nc.vector.tensor_scalar(shift_u[:, cols], ones[:], shift_b[:, b:b + 1], -1.0,
                                                  ALU.mult, ALU.mult)
                ins.then_inc(tables_ready, 1)

            def low_part(u, v):
                dve.wait_ge(u_hi_ready, u + 1)
                src = u_nrm[v % 2].rearrange("p (w c j) -> p w c j", w=2, c=CB)
                dst = u_parts[v % 4]
                nc.vector.tensor_tensor(dst[:, :, 1, :, 1:1 + J_OUT], src, dst[:, :, 0, :, 1:1 + J_OUT],
                                        ALU.subtract).then_inc(u_lo_ready, 1)

            for piece in range(2 * TILES):
                if piece == 1:
                    dve.wait_ge(const_loaded, 16 * 7)
                    nc.vector.tensor_reduce(wmax[:], w0s, AX.X, ALU.max, apply_absolute_value=True).then_inc(wmax_ready, 1)
                    dve.wait_ge(wmax_ready, 1)
                    prepare_signs()
                prepare(0, 0, piece, None, 1, channels=(0,))
                if piece == 4:
                    weights(0, 0, 1)
                if piece in (5, 6):
                    if piece == 5:
                        dve.wait_ge(split_ready, NCHUNK)
                    copy_side(0, piece - 5)

            def step(b, gi, has_next):
                g = GPB * b + gi
                for t in range(2 * TILES):
                    if has_next:
                        n = 2 * b + (gi + 1) // 2 + 1
                        prepare(g + 1, gi + 1, t, n - gi % 2, n)
                    if not has_next:
                        if t == 1:
                            tables(0, 0, EARLY)
                        if t in (6, 7):
                            low_part(t - 6, t - 6)
                    y_stats(g, gi, t)
                    if t < 2 * TILES - 2:
                        dve.wait_ge(split_ready, 2 * NCHUNK * g + NCHUNK * ((t + 2) // TILES + 1))
                        copy_side(gi, t + 2)
                    elif has_next:
                        dve.wait_ge(split_ready, 2 * NCHUNK * (g + 1) + NCHUNK)
                        copy_side(gi + 1, t + 2 - 2 * TILES)

            with dve.Fori(0, B - 1) as b:
                for gi in range(GPB):
                    step(b, gi, True)
            for gi in range(GPB):
                step(B - 1, gi, gi < GPB - 1)

            tables(1, EARLY, B)

            def unit_step(i, last):
                for v in range(UN):
                    u = UN * i + v
                    if not last or v + 2 < UN:
                        low_part(u + 2, (v + 2) % UN)
                    dve.wait_ge(u_conv_done, u + 1)
                    dve.wait_ge(stored[v % 4], CREDIT + 16 * (2 * i + v // 4))
                    nc.vector.scalar_tensor_tensor(out=yout[v % 4], in0=psum[v % 2][:].rearrange("p b e -> p (b e)"),
                                                   scalar=oscale[:], in1=yin[v], op0=ALU.mult, op1=ALU.add)\
                      .then_inc(added[v], 1)

            with dve.Fori(0, PASSES - 1) as i:
                unit_step(i, False)
            unit_step(PASSES - 1, True)


def layouts(x, w0, w1, bias):
    import numpy as np
    xp = np.pad(x, ((0, 0), (0, 0), (PAD0, PAD0), (PAD0, PAD0)), mode="reflect")
    full = np.zeros((B, C, A_IN * RB, J_IN * CB), x.dtype)
    full[:, :, :H + 2 * PAD0, :W + 2 * PAD0] = xp
    blocks = full.reshape(NCH, A_IN, RB, J_IN, CB)
    blocks = blocks.reshape(NCH, A_IN, RB, J_IN, 2, CH).transpose(0, 4, 2, 5, 1, 3)
    r0, r1, c0, c1 = RB, RB * (A_IN - 1), CB, CB * (J_IN - 2)
    y0, y1, x0, x1 = PAD0, PAD0 + H, PAD0, PAD0 + W
    rest = [xp[:, :, y0:r0, x0:x1], xp[:, :, r1:y1, x0:x1], xp[:, :, r0:r1, x0:c0], xp[:, :, r0:r1, c1:x1]]
    rest = np.concatenate([r.reshape(NCH, -1) for r in rest], axis=1)
    edge = rest.reshape(NG, GROUP_CH, P, EDGE).transpose(0, 2, 1, 3)
    half, r, c4, bi, bj, ro, co = np.meshgrid(*[np.arange(n) for n in (2, RB, CH, 2, 2, RB, CB)], indexing="ij")
    dy, dx = RB * bi + r - ro, CB * bj + CH * half + c4 - co
    whole = [d.reshape(P, 4, P) for d in (dy, dx)]
    r, c4, ro, co = np.meshgrid(*[np.arange(n) for n in (P // CH, CH, RB, CB)], indexing="ij")
    sides = [d.reshape(P, 1, P) for d in (np.where(r < R_SIDE, r - ro, -1), 2 * CB + c4 - co)]
    dy, dx = [np.concatenate([a, b], axis=1) for a, b in zip(whole, sides)]
    ok = (dy >= 0) & (dy < K0) & (dx >= 0) & (dx < K0)
    band = np.zeros((C,) + ok.shape, w0.dtype)
    band[:, ok] = w0[:, 0][:, dy[ok], dx[ok]]
    centre = ((dy == PAD0) & (dx == PAD0)).astype(np.float32)
    ri, ci, tap, ro, co = np.meshgrid(*[np.arange(n) for n in (WIN, C, 3, WIN, C)], indexing="ij")
    dy = ri - ro + 1
    ok = (dy >= 0) & (dy < 3) & (ro >= 1) & (ro <= STEP)
    band1 = np.zeros(ok.shape, w1.dtype)
    band1[ok] = w1[co[ok], ci[ok], dy[ok], tap[ok]]
    gmask = np.tile(np.arange(GPB)[None, :] == (np.arange(P) % C // GROUP_CH)[:, None], (1, B)).astype(np.float32)
    return {
        "xb": blocks.reshape(NCH, P, XCOLS), "edge": edge.reshape(NG, P, GROUP_CH * EDGE),
        "band": band.reshape(C, P, NBLK * P), "w0": w0.reshape(C, K0 * K0),
        "centre": centre.reshape(P, NBLK * P),
        "bias0": np.tile(bias, (P, B)), "band1": band1.reshape(P, 3 * P),
        "w1": np.tile(w1.reshape(C, C * 9), (WIN, 1)), "bias1": np.tile(bias.reshape(C, 1), (WIN, 1)),
        "gmask": gmask,
    }


def kernel(x, L0_conv_w, L1_conv_weight, L1_conv_bias):
    import numpy as np
    import concourse.bacc as bacc
    from concourse import mybir
    from concourse.bass_utils import run_bass_kernel_spmd

    nc = bacc.Bacc("TRN2", target_bir_lowering=False, num_devices=1)
    arrays, args = {}, []
    laid = layouts(np.asarray(x), np.asarray(L0_conv_w), np.asarray(L1_conv_weight), np.asarray(L1_conv_bias))
    for name, a in laid.items():
        a = np.ascontiguousarray(a)
        arrays["in_" + name] = a
        args.append(nc.dram_tensor("in_" + name, a.shape, mybir.dt.from_np(a.dtype), kind="ExternalInput").ap())
    F32 = mybir.dt.float32
    y1 = nc.dram_tensor("y1", (C, Q_ROWS, W), F32, kind="ExternalOutput").ap()
    y2 = nc.dram_tensor("y2", (B * RPB, C, W), F32, kind="ExternalOutput").ap()
    build(nc, *args, y1, y2)
    r = run_bass_kernel_spmd(nc, [arrays], core_ids=[0])
    out = np.asarray(r.results[0]["y2"]).reshape(B, RPB, C, CB, J_OUT)[:, :H]
    return np.ascontiguousarray(out.transpose(0, 2, 1, 4, 3)).reshape(B, C, H, W)
```
